# Optimizing a Trainium2 kernel written in Bass

```python
import numpy as np
import jax
import jax.numpy as jnp

def _softmax(x, axis=-1):
    return jax.nn.softmax(x, axis=axis)

def _gelu(x):
    return jax.nn.gelu(x, approximate=True)

def _silu(x):
    return jax.nn.silu(x)

def _sigmoid(x):
    return jax.nn.sigmoid(x)

def _layernorm(x, axis=-1, eps=1e-05):
    m = jnp.mean(x, axis=axis, keepdims=True)
    v = jnp.var(x, axis=axis, keepdims=True)
    return (x - m) / jnp.sqrt(v + eps)

def _scatter_add(tgt, idx, src, axis=0):
    return tgt.at[idx].add(src)

def _segment_sum(src, seg, n):
    return jax.ops.segment_sum(src, seg, n)
kernel_name = 'mk_hybrid_d1_jaxref_r8_bd0821'

def setup_inputs(seed: int=0):
    np.random.seed(seed)
    _w = jnp.asarray

    def _L0_attn_a_setup():
        import jax, jax.numpy as jnp
        import numpy as np
        N_HEADS = 32
        N_KV_HEADS = 8
        DIM = 512
        HEAD_DIM = DIM // N_HEADS
        N_REP = N_HEADS // N_KV_HEADS
        ROPE_THETA = 10000.0

        def _apply_rope(x):
            seq = x.shape[2]
            hd = x.shape[-1]
            inv_freq = 1.0 / ROPE_THETA ** (jnp.arange(0, hd, 2, dtype=jnp.float32) / hd)
            angles = jnp.arange(seq, dtype=jnp.float32)[:, None] * inv_freq[None, :]
            cos = jnp.cos(angles)[None, None]
            sin = jnp.sin(angles)[None, None]
            x1 = x[..., 0::2]
            x2 = x[..., 1::2]
            r1 = x1 * cos - x2 * sin
            r2 = x1 * sin + x2 * cos
            return jnp.stack([r1, r2], axis=-1).reshape(x.shape)
        key = jax.random.key(seed)
        k1, k2, k3 = jax.random.split(key, 3)
        bs, seq = (1, 256)
        x = jax.random.normal(k1, (bs, seq, DIM), dtype=jnp.float32)
        w_qkv = jax.random.normal(k2, (DIM, HEAD_DIM * (N_HEADS + 2 * N_KV_HEADS)), dtype=jnp.float32) * 0.02
        w_o = jax.random.normal(k3, (N_HEADS * HEAD_DIM, DIM), dtype=jnp.float32) * 0.02
        return {'x': x, 'w_qkv': w_qkv, 'w_o': w_o}
    _L0_attn_a_in = _L0_attn_a_setup()

    def _L0_attn_b_setup():
        import jax, jax.numpy as jnp
        import numpy as np
        DIM = 512
        N_HEADS = 32
        N_KV_HEADS = 8
        HEAD_DIM = DIM // N_HEADS
        N_REP = N_HEADS // N_KV_HEADS
        THETA = 10000.0
        B, S = (4, 128)

        def _rope_cos_sin(seq_len):
            freqs = 1.0 / THETA ** (jnp.arange(0, HEAD_DIM, 2, dtype=jnp.float32) / HEAD_DIM)
            t = jnp.arange(seq_len, dtype=jnp.float32)
            ang = jnp.outer(t, freqs)
            return (jnp.cos(ang), jnp.sin(ang))

        def _apply_rope(x, cos, sin):
            xr = x[..., 0::2]
            xi = x[..., 1::2]
            c = cos[None, :, None, :]
            s = sin[None, :, None, :]
            out_r = xr * c - xi * s
            out_i = xr * s + xi * c
            return jnp.stack([out_r, out_i], axis=-1).reshape(x.shape)
        key = jax.random.key(seed)
        ks = jax.random.split(key, 5)
        sc = 1.0 / np.sqrt(DIM).astype(np.float32)
        x = jax.random.normal(ks[0], (B, S, DIM), jnp.float32)
        wq = jax.random.normal(ks[1], (DIM, N_HEADS * HEAD_DIM), jnp.float32) * sc
        wk = jax.random.normal(ks[2], (DIM, N_KV_HEADS * HEAD_DIM), jnp.float32) * sc
        wv = jax.random.normal(ks[3], (DIM, N_KV_HEADS * HEAD_DIM), jnp.float32) * sc
        wo = jax.random.normal(ks[4], (N_HEADS * HEAD_DIM, DIM), jnp.float32) * sc
        return {'x': x, 'wq': wq, 'wk': wk, 'wv': wv, 'wo': wo}
    _L0_attn_b_in = _L0_attn_b_setup()

    def _L0_ffn_setup():
        import jax, jax.numpy as jnp
        import numpy as np
        B, S, D_IN, D_OUT = (2, 256, 512, 512)
        E, K, R = (8, 2, 16)
        SCALING = 32.0 / 16.0
        key = jax.random.key(seed)
        ks = jax.random.split(key, 6)
        x = jax.random.normal(ks[0], (B, S, D_IN), dtype=jnp.float32)
        gate_w = jax.random.normal(ks[1], (E, D_IN), dtype=jnp.float32) * 0.02
        base_w = jax.random.normal(ks[2], (D_OUT, D_IN), dtype=jnp.float32) * 0.02
        base_b = jax.random.normal(ks[3], (D_OUT,), dtype=jnp.float32) * 0.02
        lora_A = jax.random.normal(ks[4], (E, R, D_IN), dtype=jnp.float32) * 0.02
        lora_B = jax.random.normal(ks[5], (E, D_OUT, R), dtype=jnp.float32) * 0.02
        return {'x': x, 'gate_w': gate_w, 'base_w': base_w, 'base_b': base_b, 'lora_A': lora_A, 'lora_B': lora_B}
    _L0_ffn_in = _L0_ffn_setup()
    _d = {'L0_attn_a_x': _L0_attn_a_in['x'], 'L0_attn_a_w_qkv': _L0_attn_a_in['w_qkv'], 'L0_attn_a_w_o': _L0_attn_a_in['w_o'], 'L0_attn_b_wq': _L0_attn_b_in['wq'], 'L0_attn_b_wk': _L0_attn_b_in['wk'], 'L0_attn_b_wv': _L0_attn_b_in['wv'], 'L0_attn_b_wo': _L0_attn_b_in['wo'], 'L0_ffn_gate_w': _L0_ffn_in['gate_w'], 'L0_ffn_base_w': _L0_ffn_in['base_w'], 'L0_ffn_base_b': _L0_ffn_in['base_b'], 'L0_ffn_lora_A': _L0_ffn_in['lora_A'], 'L0_ffn_lora_B': _L0_ffn_in['lora_B']}
    _x0 = _d['L0_attn_a_x']
    _d['L0_attn_a_x'] = jax.random.normal(jax.random.fold_in(jax.random.key(seed), 1), (8, 256, 512), dtype=_x0.dtype)
    del _x0
    return _d

def reference(L0_attn_a_x, L0_attn_a_w_qkv, L0_attn_a_w_o, L0_attn_b_wq, L0_attn_b_wk, L0_attn_b_wv, L0_attn_b_wo, L0_ffn_gate_w, L0_ffn_base_w, L0_ffn_base_b, L0_ffn_lora_A, L0_ffn_lora_B):

    def _L0_attn_a_ref(x, w_qkv, w_o):
        import jax, jax.numpy as jnp
        import numpy as np
        N_HEADS = 32
        N_KV_HEADS = 8
        DIM = 512
        HEAD_DIM = DIM // N_HEADS
        N_REP = N_HEADS // N_KV_HEADS
        ROPE_THETA = 10000.0

        def _apply_rope(x):
            seq = x.shape[2]
            hd = x.shape[-1]
            inv_freq = 1.0 / ROPE_THETA ** (jnp.arange(0, hd, 2, dtype=jnp.float32) / hd)
            angles = jnp.arange(seq, dtype=jnp.float32)[:, None] * inv_freq[None, :]
            cos = jnp.cos(angles)[None, None]
            sin = jnp.sin(angles)[None, None]
            x1 = x[..., 0::2]
            x2 = x[..., 1::2]
            r1 = x1 * cos - x2 * sin
            r2 = x1 * sin + x2 * cos
            return jnp.stack([r1, r2], axis=-1).reshape(x.shape)
        bs, seq, _ = x.shape
        qkv = x @ w_qkv
        q_sz = N_HEADS * HEAD_DIM
        kv_sz = N_KV_HEADS * HEAD_DIM
        xq = qkv[..., :q_sz].reshape(bs, seq, N_HEADS, HEAD_DIM).transpose(0, 2, 1, 3)
        xk = qkv[..., q_sz:q_sz + kv_sz].reshape(bs, seq, N_KV_HEADS, HEAD_DIM).transpose(0, 2, 1, 3)
        xv = qkv[..., q_sz + kv_sz:].reshape(bs, seq, N_KV_HEADS, HEAD_DIM).transpose(0, 2, 1, 3)
        xq = _apply_rope(xq)
        xk = _apply_rope(xk)
        keys = jnp.repeat(xk, N_REP, axis=1)
        values = jnp.repeat(xv, N_REP, axis=1)
        scale = 1.0 / jnp.sqrt(jnp.float32(HEAD_DIM))
        scores = jnp.einsum('bhsd,bhtd->bhst', xq, keys) * scale
        causal = jnp.tril(jnp.ones((seq, seq), dtype=bool))[None, None]
        scores = jnp.where(causal, scores, -jnp.inf)
        probs = jax.nn.softmax(scores, axis=-1)
        out = jnp.einsum('bhst,bhtd->bhsd', probs, values)
        out = out.transpose(0, 2, 1, 3).reshape(bs, seq, N_HEADS * HEAD_DIM)
        return out @ w_o

    def _L0_attn_b_ref(x, wq, wk, wv, wo):
        import jax, jax.numpy as jnp
        import numpy as np
        DIM = 512
        N_HEADS = 32
        N_KV_HEADS = 8
        HEAD_DIM = DIM // N_HEADS
        N_REP = N_HEADS // N_KV_HEADS
        THETA = 10000.0
        B, S = (4, 128)

        def _rope_cos_sin(seq_len):
            freqs = 1.0 / THETA ** (jnp.arange(0, HEAD_DIM, 2, dtype=jnp.float32) / HEAD_DIM)
            t = jnp.arange(seq_len, dtype=jnp.float32)
            ang = jnp.outer(t, freqs)
            return (jnp.cos(ang), jnp.sin(ang))

        def _apply_rope(x, cos, sin):
            xr = x[..., 0::2]
            xi = x[..., 1::2]
            c = cos[None, :, None, :]
            s = sin[None, :, None, :]
            out_r = xr * c - xi * s
            out_i = xr * s + xi * c
            return jnp.stack([out_r, out_i], axis=-1).reshape(x.shape)
        bsz, seq_len, _ = x.shape
        q = (x @ wq).reshape(bsz, seq_len, N_HEADS, HEAD_DIM)
        k = (x @ wk).reshape(bsz, seq_len, N_KV_HEADS, HEAD_DIM)
        v = (x @ wv).reshape(bsz, seq_len, N_KV_HEADS, HEAD_DIM)
        cos, sin = _rope_cos_sin(seq_len)
        q = _apply_rope(q, cos, sin)
        k = _apply_rope(k, cos, sin)
        k = jnp.repeat(k, N_REP, axis=2)
        v = jnp.repeat(v, N_REP, axis=2)
        scores = jnp.einsum('bqhd,bkhd->bhqk', q, k) / np.float32(np.sqrt(HEAD_DIM))
        mask = jnp.triu(jnp.full((seq_len, seq_len), -jnp.inf, dtype=scores.dtype), k=1)
        scores = scores + mask
        attn = jax.nn.softmax(scores.astype(jnp.float32), axis=-1).astype(q.dtype)
        out = jnp.einsum('bhqk,bkhd->bqhd', attn, v).reshape(bsz, seq_len, N_HEADS * HEAD_DIM)
        return out @ wo

    def _L0_ffn_ref(x, gate_w, base_w, base_b, lora_A, lora_B):
        import jax, jax.numpy as jnp
        import numpy as np
        B, S, D_IN, D_OUT = (2, 256, 512, 512)
        E, K, R = (8, 2, 16)
        SCALING = 32.0 / 16.0
        gate_logits = jnp.einsum('bsd,ed->bse', x, gate_w)
        weights, selected = jax.lax.top_k(gate_logits, K)
        weights = jax.nn.softmax(weights.astype(jnp.float32), axis=2).astype(x.dtype)
        result = jnp.einsum('bsd,od->bso', x, base_w) + base_b
        w_full = jnp.sum(jax.nn.one_hot(selected, E, dtype=x.dtype) * weights[..., None], axis=2)
        low = jnp.einsum('bsd,erd->ebsr', x, lora_A)
        lora_out = jnp.einsum('ebsr,eor,bse->bso', low, lora_B, w_full)
        result = result + SCALING * lora_out
        return result
    x = L0_attn_a_x
    x = x + _L0_attn_a_ref(_layernorm(x, axis=-1), L0_attn_a_w_qkv, L0_attn_a_w_o)
    x = x + _L0_ffn_ref(_layernorm(x, axis=-1), L0_ffn_gate_w, L0_ffn_base_w, L0_ffn_base_b, L0_ffn_lora_A, L0_ffn_lora_B)
    x = x + _L0_attn_b_ref(_layernorm(x, axis=-1), L0_attn_b_wq, L0_attn_b_wk, L0_attn_b_wv, L0_attn_b_wo)
    x = x + _L0_ffn_ref(_layernorm(x, axis=-1), L0_ffn_gate_w, L0_ffn_base_w, L0_ffn_base_b, L0_ffn_lora_A, L0_ffn_lora_B)
    return x

_drawn_inputs = setup_inputs


def setup_inputs(seed=0):
    import zlib

    import numpy as np

    out = dict(_drawn_inputs(seed))
    spreads = {}
    factors = {}
    for name, (base, spread) in spreads.items():
        noise = np.random.default_rng([zlib.crc32(name.encode()), seed]).standard_normal(out[name].shape)
        drawn = base * np.exp(spread * noise) if base else spread * noise
        out[name] = jnp.asarray(drawn.astype(out[name].dtype))
    for name, factor in factors.items():
        out[name] = (out[name] * factor).astype(out[name].dtype)
    return out
```

```python
from contextlib import ExitStack

import concourse.bass as bass
from concourse import mybir

F32 = mybir.dt.float32
F32R = mybir.dt.float32r
BF16 = mybir.dt.bfloat16
U32 = mybir.dt.uint32
ALU = mybir.AluOpType
ACT = mybir.ActivationFunctionType
AX = mybir.AxisListType

P = 128
D = 512
NT = 16
NB = 8
NL = 2
SLOTS = NL * NB
EPS = 1e-5
SCALING = 2.0


def plan():
    prog = []

    def add(*item):
        prog.append(item)

    def pre(s, *names):
        if s < SLOTS:
            for n in names:
                if n[:2] in ("aT", "aM", "aR", "aH"):
                    add(n[:2], 2 * s + int(n[2]))
                elif n == "aL":
                    add("aL", s)
                elif n in ("aS0", "aS1"):
                    for i in range(5):
                        add("aS", 2 * s + int(n[2]), i)

    def post(s, *names):
        if s >= 0:
            for n in names:
                if n in ("fL", "fG", "fW"):
                    add(n, s)
                else:
                    add(n[:2], 2 * s + int(n[2]))

    wk = iter(range(25))

    def weights(n):
        for _ in range(n):
            add("W", next(wk))

    weights(4)
    pre(0, "aL", "aT0", "aM0", "aR0", "aT1", "aH0", "aM1", "aR1", "aS0", "aH1", "aS1")
    pre(1, "aL", "aT0")
    for s in range(SLOTS + 1):
        for g in range(8):
            u = 8 * s + g
            live = s < SLOTS
            if live:
                add("S", u)
            if g % 2 == 0 and u >= 2:
                if live or g == 0:
                    add("PV", u // 2 - 1)
            if g % 2 == 1 and u >= 3 and (live or g == 1):
                add("OT", (u - 1) // 2 - 1)
            if g == 0:
                pre(s + 1, "aM0", "aR0", "aT1", "aH0")
            if g == 1:
                pre(s + 1, "aM1", "aR1")
            if g == 2:
                post(s - 1, "oT0", "oT1")
                pre(s + 1, "aS0")
            if g == 3:
                pre(s + 1, "aH1")
                post(s - 1, "oM0", "oM1")
            if g == 4:
                post(s - 1, "fL")
                pre(s + 1, "aS1")
            if g == 5:
                post(s - 1, "fT0", "fT1", "fA0")
            if g == 6:
                post(s - 1, "fA1", "fG", "fB0")
                pre(s + 2, "aL")
            if s == 0:
                weights((2, 2, 2, 2, 2, 2, 1, 0)[g])
            if s in (6, 8) and g in (4, 5, 6, 7):
                weights(1)
            if live:
                add("PT", u, 0)
                add("PT", u, 1)
            if g == 7:
                post(s - 1, "fB1", "fW")
                pre(s + 2, "aT0")
                post(s - 1, "fC0", "fC1")
            if live:
                add("PT", u, 2)
    return prog


def hybrid_block_kernel(nc, x_in, wqa, woa, wqb, wob, wg, wb, wl, bias_in, trig_in, iden_in, idb_in,
                        mask_in, iota_in, out):
    prog = plan()

    tuse, guse, xuse = {}, {}, {}
    tfree, gfree, xfree = [], [], []
    for item in prog:
        k = item[0]
        if k in ("aT", "oT", "fT"):
            tuse[item] = len(tfree)
            tfree.append((k[0] + "l", item[1]))
            xuse[(k[0], item[1])] = len(xfree)
            xfree.append(({"a": "aK", "o": "oM", "f": "fB"}[k[0]], item[1]))
        elif k == "aS":
            tuse[item] = len(tfree)
            n, i = item[1:]
            tfree.append(("kt", n) if i == 0 else (("qa", 2 * n + (i - 2) // 2) if i % 2 == 0 else
                                                  ("qd", 2 * n + (i - 1) // 2)))
        elif k == "PT":
            tuse[item] = len(tfree)
            tfree.append(("p" + "abc"[item[2]], item[1]))
        elif k == "OT":
            tuse[item] = len(tfree)
            tfree.append(("on", item[1]))
        elif k == "fW":
            tuse[item] = len(tfree)
            tfree.append(("wl", item[1]))
        elif k == "aM":
            guse[("aQ", item[1])] = len(gfree)
            gfree.append(("uq", item[1]))
            guse[("aK", item[1])] = len(gfree)
            gfree.append(("av", item[1]))
        elif k == "oM":
            guse[("oM", item[1])] = len(gfree)
            gfree.append(("ox", item[1]))
        elif k == "fA":
            guse[("fA", item[1])] = len(gfree)
            gfree.append(("fg", item[1]))
        elif k == "fB":
            guse[("fB", item[1])] = len(gfree)
            gfree.append(("fx", item[1]))

    with ExitStack() as ctx:
        def sb(name, shape, dt):
            return ctx.enter_context(nc.sbuf_tensor(name, shape, dt))

        def pb(name, shape):
            return ctx.enter_context(nc.psum_tensor(name, shape, F32))

        X = sb("X", [P, NT, D], F32)
        Wst = sb("Wst", [P, 2, 768], F32)
        WQh = sb("WQh", [P, 4, 768], F32R)
        WQl = sb("WQl", [P, 4, 768], F32R)
        WOh = sb("WOh", [P, 4, D], F32R)
        WOl = sb("WOl", [P, 4, D], F32R)
        WGh = sb("WGh", [P, 4, 136], F32R)
        WGl = sb("WGl", [P, 4, 136], F32R)
        WBh = sb("WBh", [P, 4, D], F32R)
        WBl = sb("WBl", [P, 4, D], F32R)
        WLh = sb("WLh", [P, D], F32R)
        WLl = sb("WLl", [P, D], F32R)
        xn = sb("xn", [P, 2, D], F32)
        at = sb("at", [P, 2, D], F32)
        XH = sb("XH", [P, 2, D], F32R)
        XL = sb("XL", [P, 2, D], F32R)
        U1 = sb("U1", [P, 2, 40, 8], F32)
        U2 = sb("U2", [P, 2, 40, 8], F32)
        Sst = sb("Sst", [P, 40, 64], F32R)
        QT = sb("QT", [P, 2, 4, 4, 2, 128], F32R)
        KT = sb("KT", [P, 2, 4, 256], F32R)
        V = sb("V", [P, 2, 2, 8, 32], F32)
        P0 = sb("P0", [P, 4, 128], F32)
        P1 = sb("P1", [P, 4, 256], F32)
        PTs = sb("PTs", [P, 2, 3, 512], F32)
        Os = sb("Os", [P, 512], F32)
        rc = sb("rc", [P, 16], F32)
        nm = sb("nm", [P, 2, 8], F32)
        st6 = sb("st6", [P, 2, 2, 6], F32)
        mv = sb("mv", [P, 2, 2, 2], F32)
        ve = sb("ve", [P, 2, 2], F32)
        rs = sb("rs", [P, 2, 2], F32)
        mh = sb("mh", [P, 2], F32)
        glo = sb("glo", [P, 2, 136], F32)
        mx = sb("mx", [P, 2, 8], F32)
        mi = sb("mi", [P, 2, 8], U32)
        gd = sb("gd", [P, 2], F32)
        gx = sb("gx", [P, 2], F32)
        gn = sb("gn", [P, 2], F32)
        wsel = sb("wsel", [P, 2, 2], F32)
        mif = sb("mif", [P, 2, 2], F32)
        t1 = sb("t1", [P, 2, 8], F32)
        t2 = sb("t2", [P, 2, 8], F32)
        wf = sb("wf", [P, 2, 8], F32)
        lw = sb("lw", [P, 2, 128], F32)
        LH = sb("LH", [P, 256], F32R)
        LL = sb("LL", [P, 256], F32R)
        bias = sb("bias", [P, D], F32)
        trig = sb("trig", [P, 2, 4, 8], F32)
        iden = sb("iden", [P, 128], F32)
        idb = sb("idb", [P, 128], BF16)
        mask = sb("mask", [P, 512], BF16)
        iota = sb("iota", [P, 8], F32)

        S0 = pb("S0", [P, 4, 128])
        S1 = pb("S1", [P, 4, 256])
        T = [pb(f"T{i}", [P, 512]) for i in range(2)]
        O = pb("O", [P, 512])
        G = [pb(f"G{i}", [P, 512]) for i in range(2)]

        sems, made, known = {}, {}, {}

        def sem(name):
            if name not in sems:
                sems[name] = ctx.enter_context(nc.semaphore("s_" + name))
            return sems[name]

        def done(ins, name, n):
            assert made.get(name, 0) == n, (name, n, made.get(name))
            made[name] = n + 1
            ins.then_inc(sem(name), 1)

        def need(e, name, n, step=1):
            v = step * (n + 1)
            if n >= 0 and known.get((id(e), name), 0) < v:
                known[(id(e), name)] = v
                e.wait_ge(sem(name), v)

        def tbank(e, item):
            k = tuse[item]
            if k >= 2:
                need(e, *tfree[k - 2])
            return T[k % 2]

        def tb(item):
            return T[tuse[item] % 2]

        def gbank(e, key):
            k = guse[key]
            if k >= 2:
                need(e, *gfree[k - 2])
            return G[k % 2]

        def gb(key):
            return G[guse[key] % 2]

        def cols(dram, c, n):
            return dram[c * P:(c + 1) * P, 0:n]

        wch = []
        for c in range(4):
            wch.append((cols(wqa, c, 768), WQh[:, c, :], WQl[:, c, :], 768))
        for c in range(4):
            wch.append((cols(woa, c, D), WOh[:, c, :], WOl[:, c, :], D))
        for c in range(4):
            wch.append((cols(wg, c, 136), WGh[:, c, :], WGl[:, c, :], 136))
        for c in range(4):
            wch.append((cols(wb, c, D), WBh[:, c, :], WBl[:, c, :], D))
        wch.append((cols(wl, 0, D), WLh[:, :], WLl[:, :], D))
        for c in range(4):
            wch.append((cols(wqb, c, 768), WQh[:, c, :], WQl[:, c, :], 768))
        for c in range(4):
            wch.append((cols(wob, c, D), WOh[:, c, :], WOl[:, c, :], D))
        wland = [PTs[:, k // 2, :, :].rearrange("p a b -> p (a b)")[:, (k % 2) * 768:(k % 2 + 1) * 768]
                 if k < 4 else Wst[:, k % 2, 0:wch[k][3]] for k in range(len(wch))]

        names = [it[1] for it in prog if it[0] == "W"]
        nw = len(wch)
        assert names[:nw] == list(range(nw))

        def wlanded(e, k):
            if k < 4:
                need(e, f"wf{k}", 0, 16)
            else:
                need(e, f"wd{k % 2}", (k - 4) // 2, 16)

        block = ctx.enter_context(nc.Block())

        @block.sync
        def _(e):
            def load(dst, src, name):
                e.dma_start(dst, src).then_inc(sem(name), 16)

            def xload(b):
                load(X[:, 2 * b:2 * b + 2, :],
                     x_in[256 * b:256 * b + 256, :].rearrange("(t p) d -> p t d", p=P), f"x{b}")

            xload(0)
            load(iden[:, :], iden_in, "c_id")
            load(wland[0], wch[0][0], "wf0")
            load(wland[1], wch[1][0], "wf1")
            load(trig[:, :, :, :].rearrange("p a b c -> p (a b c)"), trig_in, "c_trig")
            load(wland[2], wch[2][0], "wf2")
            load(wland[3], wch[3][0], "wf3")
            load(mask[:, :], mask_in, "c_mask")
            load(idb[:, :], idb_in, "c_idb")
            for b in range(1, NB):
                xload(b)
            load(bias[:, :], bias_in, "c_bias")
            load(iota[:, :], iota_in, "c_iota")
            for k in range(4, nw):
                if k >= 6:
                    need(e, "wlo", k - 2)
                load(wland[k], wch[k][0], f"wd{k % 2}")
            for n in range(NT):
                need(e, "fx", NT + n)
                e.dma_start(out[n * P:(n + 1) * P, :], X[:, n, :]).then_inc(sem("out"), 16)
            e.wait_ge(sem("out"), 16 * NT)


        @block.tensor
        def _(e):
            def front(c, n):
                item = (c + "T", n)
                if c == "o":
                    need(e, "on", 4 * (n // 2) + 3)
                    src = at[:, n % 2, :]
                else:
                    need(e, c + "xn", n)
                    src = xn[:, n % 2, :]
                need(e, "c_id", 0, 16)
                t = tbank(e, item)
                for k in range(4):
                    ins = e.transpose(t[:, k * P:(k + 1) * P], src[:, k * P:(k + 1) * P], iden[:, :])
                done(ins, c + "t", n)

            def proj(c, n, bank, wh, wlo, first=True, last=True):
                k = xuse[(c, n)] % 2
                need(e, c + "h", n)
                need(e, c + "l", n)
                for j in range(4):
                    xh = XH[:, k, j * P:(j + 1) * P]
                    xl = XL[:, k, j * P:(j + 1) * P]
                    e.matmul(bank, xh, wh(j), start=(first and j == 0), stop=False, skip_group_check=True)
                    e.matmul(bank, xh, wlo(j), start=False, stop=False, skip_group_check=True)
                    ins = e.matmul(bank, xl, wh(j), start=False, stop=(last and j == 3),
                                   skip_group_check=True)
                return ins

            def v_aM(n):
                need(e, "wlo", 3 if n < 16 else 20)
                g = gbank(e, ("aQ", n))
                done(proj("a", n, g[:, :], lambda j: WQh[:, j, 0:512], lambda j: WQl[:, j, 0:512]), "aQ", n)
                g = gbank(e, ("aK", n))
                done(proj("a", n, g[:, 0:256], lambda j: WQh[:, j, 512:768], lambda j: WQl[:, j, 512:768]),
                     "aK", n)

            def v_aS(n, i):
                t = tbank(e, ("aS", n, i))
                for name in ("hq1", "lq", "lk"):
                    need(e, name, n)
                for j in range(4):
                    h = 32 + 2 * j if i == 0 else (i - 1) * 8 + 2 * j
                    src = Sst[:, h:h + 2, :].rearrange("p a b -> p (a b)").bitcast(F32)
                    ins = e.transpose(t[:, j * P:(j + 1) * P], src, iden[:, :])
                done(ins, "st", 5 * n + i)

            def v_S(u):
                s, g = divmod(u, 8)
                gg, r0 = g // 2, 64 * (g % 2)
                b = s % 2
                need(e, "c_mask", 0, 16)
                need(e, "c_idb", 0, 16)
                for n in (2 * s, 2 * s + 1):
                    need(e, "kt", n)
                    if gg % 2 == 0:
                        need(e, "qd", 2 * n + gg // 2)
                    else:
                        need(e, "qa", 2 * n + gg // 2)
                need(e, "e0", u - 1)
                e.matmul(S0[:, :, :].rearrange("p a b -> p (a b)"), idb[:, :], mask[:, :],
                         start=True, stop=False, skip_group_check=True)
                for j in range(4):
                    ins = e.matmul(S0[:, j, :], QT[r0:r0 + 48, b, gg, j, 0, :], KT[r0:r0 + 48, b, gg, 0:128],
                                   start=False, stop=True, skip_group_check=True)
                done(ins, "s0", u)
                need(e, "e1", u - 1)
                for h in range(2):
                    e.matmul(S1[:, 2 * h:2 * h + 2, 128:256], idb[:, :],
                             mask[:, 0:256].rearrange("p (a b) -> p a b", a=2),
                             start=True, stop=False, skip_group_check=True)
                for j in range(4):
                    ins = e.matmul(S1[:, j, :], QT[r0:r0 + 48, b, gg, j, 1, :], KT[r0:r0 + 48, b, gg, :],
                                   start=False, stop=True, skip_group_check=True)
                done(ins, "s1", u)

            def v_PT(u, i):
                need(e, "e0" if i == 0 else "e1", u)
                t = tbank(e, ("PT", u, i))
                for j in range(4):
                    src = P0[:, j, :] if i == 0 else P1[:, j, (i - 1) * P:i * P]
                    ins = e.transpose(t[:, j * P:(j + 1) * P], src, iden[:, :])
                done(ins, "pt", 3 * u + i)

            def v_PV(p):
                s = p // 4
                for u in (2 * p, 2 * p + 1):
                    for i in "abc":
                        need(e, "p" + i, u)
                need(e, "av", 2 * s + 1)
                need(e, "vinit", 0)
                need(e, "oc", p - 1)
                for u in (2 * p, 2 * p + 1):
                    g, q = u % 8, 64 * (u % 2)
                    e.matmul(O[q:q + 32, :], V[:, s % 2, 0, g, :], PTs[:, u % 2, 0, :],
                             start=True, stop=True, skip_group_check=True)
                    e.matmul(O[q + 32:q + 64, :], V[:, s % 2, 0, g, :], PTs[:, u % 2, 1, :],
                             start=True, stop=False, skip_group_check=True)
                for u in (2 * p, 2 * p + 1):
                    g, q = u % 8, 64 * (u % 2)
                    ins = e.matmul(O[q + 32:q + 64, :], V[:, s % 2, 1, g, :], PTs[:, u % 2, 2, :],
                                   start=False, stop=True, skip_group_check=True)
                done(ins, "pv", p)

            def v_OT(p):
                need(e, "oc", p)
                t = tbank(e, ("OT", p))
                for j in range(4):
                    ins = e.transpose(t[:, j * P:(j + 1) * P], Os[:, j * P:(j + 1) * P], iden[:, :])
                done(ins, "oT", p)

            def v_oM(n):
                need(e, "wlo", 7 if n < 16 else 24)
                g = gbank(e, ("oM", n))
                done(proj("o", n, g[:, :], lambda j: WOh[:, j, :], lambda j: WOl[:, j, :]), "oM", n)

            def v_fA(n):
                need(e, "wlo", 11)
                g = gbank(e, ("fA", n))
                done(proj("f", n, g[:, 0:136], lambda j: WGh[:, j, :], lambda j: WGl[:, j, :]), "fA", n)

            def v_fB(n):
                need(e, "wlo", 15)
                g = gbank(e, ("fB", n))
                done(proj("f", n, g[:, :], lambda j: WBh[:, j, :], lambda j: WBl[:, j, :], last=False),
                     "fB", n)

            def v_fW(s):
                t = tbank(e, ("fW", s))
                for i in range(2):
                    need(e, "lw", 2 * s + i)
                    ins = e.transpose(t[:, i * P:(i + 1) * P], lw[:, i, :], iden[:, :])
                done(ins, "wt", s)

            def v_fC(n):
                need(e, "wlo", 16)
                need(e, "wh", n // 2)
                need(e, "wl", n // 2)
                g = gb(("fB", n))
                i = n % 2
                e.matmul(g[:, :], LH[:, i * P:(i + 1) * P], WLh[:, :], start=False, stop=False,
                         skip_group_check=True)
                e.matmul(g[:, :], LH[:, i * P:(i + 1) * P], WLl[:, :], start=False, stop=False,
                         skip_group_check=True)
                done(e.matmul(g[:, :], LL[:, i * P:(i + 1) * P], WLh[:, :], start=False, stop=True,
                              skip_group_check=True), "fC", n)

            for item in prog:
                k, a = item[0], item[1:]
                if k in ("aT", "oT", "fT"):
                    front(k[0], *a)
                elif k == "aM":
                    v_aM(*a)
                elif k == "aS":
                    v_aS(*a)
                elif k == "S":
                    v_S(*a)
                elif k == "PT":
                    v_PT(*a)
                elif k == "PV":
                    v_PV(*a)
                elif k == "OT":
                    v_OT(*a)
                elif k == "oM":
                    v_oM(*a)
                elif k == "fA":
                    v_fA(*a)
                elif k == "fB":
                    v_fB(*a)
                elif k == "fW":
                    v_fW(*a)
                elif k == "fC":
                    v_fC(*a)

        @block.scalar
        def _(e):
            def copy(dst, src):
                return e.activation(dst, src, ACT.Copy)

            def front_h(c, n):
                k = xuse[(c, n)]
                need(e, c + "t", n)
                if k >= 2:
                    need(e, *xfree[k - 2])
                done(copy(XH[:, k % 2, :], tb((c + "T", n))[:, :]), c + "h", n)

            def s_W(k):
                if k >= nw:
                    return
                wlanded(e, k)
                if 17 <= k < 21:
                    need(e, "aK", 15)
                if 21 <= k:
                    need(e, "oM", 15)
                n = wch[k][3]
                done(copy(wch[k][1], wland[k]), "whi", k)

            def s_aR(n):
                need(e, "uk", n)
                s = n // 2
                if s >= 2:
                    need(e, "pv", 4 * (s - 2) + 3)
                need(e, "vinit", 0)
                done(copy(V[:, s % 2, n % 2, :, 0:16],
                          gb(("aK", n))[:, 128:256].rearrange("p (g d) -> p g d", d=16)), "av", n)

            def s_aH(n):
                need(e, "ro", n)
                need(e, "st", 5 * (n - 1) + 4)
                need(e, "sinit", 0)
                for r in range(2):
                    done(copy(Sst[:, 0:32, 32 * r:32 * r + 16].rearrange("p a (h f) -> p h a f", h=2),
                              U1[:, :, 0:32, :]), f"hq{r}", n)
                for r in range(2):
                    done(copy(Sst[:, 32:40, 16 * r:16 * r + 16].rearrange("p a (h f) -> p h a f", h=2),
                              U1[:, :, 32:40, :]), f"hk{r}", n)

            def s_aS(n, i):
                if i in (0, 2, 4):
                    t = tb(("aS", n, i))
                    s, q = divmod(n, 2)
                    need(e, "st", 5 * n + i)
                    if i == 0:
                        if s >= 2:
                            need(e, "s1", 8 * (s - 2) + 7)
                        done(copy(KT[:, s % 2, :, q * P:(q + 1) * P],
                                  t[:, :].rearrange("p (g k) -> p g k", g=4)), "kt", n)
                    else:
                        if s >= 2:
                            need(e, "s1", 8 * (s - 2) + 7)
                        done(copy(QT[:, s % 2, i - 1, :, q, :],
                                  t[:, :].rearrange("p (g k) -> p g k", g=4)), "qa", 2 * n + (i - 2) // 2)

            def s_S(u):
                need(e, "m0", u)
                need(e, "pt", 3 * (u - 1) + 0)
                for j in range(4):
                    ins = e.activation(P0[:, j, :], S0[:, j, :], ACT.Exp, bias=nm[:, u % 2, j:j + 1])
                done(ins, "e0", u)
                need(e, "m1", u)
                need(e, "pt", 3 * (u - 1) + 2)
                for j in range(4):
                    ins = e.activation(P1[:, j, :], S1[:, j, :], ACT.Exp, bias=nm[:, u % 2, 4 + j:5 + j])
                done(ins, "e1", u)

            def s_PT(u, i):
                if i == 1:
                    return
                need(e, "pt", 3 * u + i)
                if u >= 2:
                    need(e, "pv", (u - 2) // 2)
                else:
                    need(e, "wlo", 3)
                done(copy(PTs[:, u % 2, i, :], tb(("PT", u, i))[:, :]), "p" + "abc"[i], u)

            def s_PV(p):
                need(e, "pv", p)
                need(e, "oT", p - 1)
                done(copy(Os[:, :], O[:, :]), "oc", p)

            def s_fA(n):
                need(e, "fA", n)
                need(e, "lw", n - 2)
                done(copy(glo[:, n % 2, :], gb(("fA", n))[:, 0:136]), "fg", n)

            def s_fG(s):
                need(e, "gd", s)
                done(e.activation(gx[:, :], gd[:, :], ACT.Exp), "gx", s)

            def s_fW(s):
                need(e, "wt", s)
                need(e, "fC", 2 * s - 1)
                done(copy(LH[:, :], tb(("fW", s))[:, 0:256]), "wh", s)

            for item in prog:
                k, a = item[0], item[1:]
                if k == "W":
                    s_W(*a)
                elif k in ("aT", "oT", "fT"):
                    front_h(k[0], *a)
                elif k == "aR":
                    s_aR(*a)
                elif k == "aH":
                    s_aH(*a)
                elif k == "aS":
                    s_aS(*a)
                elif k == "S":
                    s_S(*a)
                elif k == "PT":
                    s_PT(*a)
                elif k == "PV":
                    s_PV(*a)
                elif k == "fA":
                    s_fA(*a)
                elif k == "fG":
                    s_fG(*a)
                elif k == "fW":
                    s_fW(*a)

        @block.vector
        def _(e):
            def front_l(c, n):
                k = xuse[(c, n)]
                need(e, c + "h", n)
                if k >= 2:
                    need(e, *xfree[k - 2])
                done(e.tensor_tensor(XL[:, k % 2, :], tb((c + "T", n))[:, :], XH[:, k % 2, :].bitcast(F32),
                                     ALU.subtract), c + "l", n)

            def v_W(k):
                if k >= nw:
                    return
                need(e, "whi", k)
                if 17 <= k < 21:
                    need(e, "aK", 15)
                if 21 <= k:
                    need(e, "oM", 15)
                done(e.tensor_tensor(wch[k][2], wland[k], wch[k][1].bitcast(F32), ALU.subtract), "wlo", k)

            def ln(c, s):
                w = 0 if c == "a" else 1
                if c == "a":
                    if s < NB:
                        need(e, f"x{s}", 0, 16)
                    else:
                        need(e, "fx", 2 * (s - NB) + 1)
                else:
                    need(e, "ox", 2 * s + 1)
                for i in range(2):
                    t = (2 * s + i) % NT
                    done(e.bn_stats(st6[:, w, i, :], X[:, t, :]), "nb" + c, 2 * s + i)
                for i in range(2):
                    need(e, "nb" + c, 2 * s + i)
                    done(e.bn_aggr(mv[:, w, i, :], st6[:, w, i, :]), "ng" + c, 2 * s + i)
                need(e, "ng" + c, 2 * s + 1)
                need(e, "np" + c, s - 1)
                done(e.tensor_scalar(ve[:, w, :], mv[:, w, :, 1], EPS, None, ALU.add), "ne" + c, s)
                need(e, "np" + c, s)
                for i in range(2):
                    n = 2 * s + i
                    t = n % NT
                    need(e, lnfree[(c, s)][0], lnfree[(c, s)][1] + i)
                    done(e.tensor_scalar(xn[:, i, :], X[:, t, :], mv[:, w, i, 0:1], rs[:, w, i:i + 1],
                                         ALU.subtract, ALU.mult), c + "xn", n)

            lnfree, last = {}, None
            for it in prog:
                if it[0] in ("aL", "fL"):
                    lnfree[(it[0][0], it[1])] = (last[0] + "t", 2 * last[1]) if last else ("at", -2)
                    last = (it[0][0], it[1])

            def v_aR(n):
                q = n % 2
                need(e, "c_trig", 0, 16)
                need(e, "aQ", n)
                need(e, "hk1", n - 1)
                need(e, "lk", n - 1)
                g = gb(("aQ", n))[:, :].rearrange("p (h a f) -> p h a f", h=2, f=8)

                def tr(i, h):
                    return trig[:, q, i, :].unsqueeze(1).unsqueeze(1).to_broadcast([P, 2, h, 8])

                e.tensor_tensor(U1[:, :, 0:32, :], g, tr(0, 32), ALU.mult)
                done(e.tensor_tensor(U2[:, :, 0:32, :], g, tr(1, 32), ALU.mult), "uq", n)
                need(e, "aK", n)
                g = gb(("aK", n))[:, 0:128].rearrange("p (h a f) -> p h a f", h=2, f=8)
                e.tensor_tensor(U1[:, :, 32:40, :], g, tr(2, 8), ALU.mult)
                done(e.tensor_tensor(U2[:, :, 32:40, :], g, tr(3, 8), ALU.mult), "uk", n)
                need(e, "uk", n)
                e.tensor_tensor(U1[:, 0, :, :], U1[:, 0, :, :], U2[:, 1, :, :], ALU.subtract)
                done(e.tensor_tensor(U1[:, 1, :, :], U1[:, 1, :, :], U2[:, 0, :, :], ALU.add), "ro", n)

            def v_aH(n):
                need(e, "ro", n)
                need(e, "hq0", n)
                done(e.tensor_tensor(Sst[:, 0:32, 16:32].rearrange("p a (h f) -> p h a f", h=2),
                                     U1[:, :, 0:32, :],
                                     Sst[:, 0:32, 0:16].rearrange("p a (h f) -> p h a f", h=2).bitcast(F32),
                                     ALU.subtract), "lq", n)
                need(e, "hk0", n)
                need(e, "hk1", n)
                done(e.tensor_tensor(Sst[:, 32:40, 32:48].rearrange("p a (h f) -> p h a f", h=2),
                                     U1[:, :, 32:40, :],
                                     Sst[:, 32:40, 0:16].rearrange("p a (h f) -> p h a f", h=2).bitcast(F32),
                                     ALU.subtract), "lk", n)
                need(e, "lq", n)
                need(e, "lk", n)

            def v_aS(n, i):
                if i in (1, 3):
                    t = tb(("aS", n, i))
                    s, q = divmod(n, 2)
                    need(e, "st", 5 * n + i)
                    if s >= 2:
                        need(e, "s1", 8 * (s - 2) + 7)
                    done(e.tensor_copy(QT[:, s % 2, i - 1, :, q, :],
                                       t[:, :].rearrange("p (g k) -> p g k", g=4)), "qd", 2 * n + (i - 1) // 2)

            def v_S(u):
                need(e, "s0", u)
                need(e, "e1", u - 2)
                done(e.tensor_reduce(nm[:, u % 2, 0:4], S0[:, :, :], AX.X, ALU.max, negate=True), "m0", u)
                need(e, "s1", u)
                done(e.tensor_reduce(nm[:, u % 2, 4:8], S1[:, :, :], AX.X, ALU.max, negate=True), "m1", u)

            def v_PT(u, i):
                if i != 1:
                    return
                need(e, "pt", 3 * u + i)
                if u >= 2:
                    need(e, "pv", (u - 2) // 2)
                else:
                    need(e, "wlo", 3)
                done(e.tensor_copy(PTs[:, u % 2, i, :], tb(("PT", u, i))[:, :]), "pb", u)

            def v_OT(p):
                s, gg = divmod(p, 4)
                need(e, "oT", p)
                need(e, "ot", 2 * s - 1)
                t = tb(("OT", p))[:, :].rearrange("p (j a q d) -> p j a q d", j=4, a=2, q=2)
                need(e, "on", p - 1)
                done(e.reciprocal(rc[:, :].rearrange("p (j a q) -> p j a q", j=4, a=2), t[:, :, :, :, 16]),
                     "rc", p)
                need(e, "rc", p)
                for q in range(2):
                    dst = at[:, q, gg * 128:(gg + 1) * 128].rearrange("p (a j d) -> p j a d", a=2, j=4)
                    rb = rc[:, :].rearrange("p (j a q) -> p j a q", j=4, a=2)[:, :, :, q]
                    ins = e.tensor_tensor(dst, t[:, :, :, q, 0:16],
                                          rb.unsqueeze(3).to_broadcast([P, 4, 2, 16]), ALU.mult)
                done(ins, "on", p)

            def v_oM(n):
                t = n % NT
                need(e, "oM", n)
                done(e.tensor_tensor(X[:, t, :], gb(("oM", n))[:, :], X[:, t, :], ALU.add), "ox", n)

            def v_fG(s):
                need(e, "c_iota", 0, 16)
                for i in range(2):
                    n = 2 * s + i
                    need(e, "fg", n)
                    lg = glo[:, i, 128:136]
                    done(e.max(mx[:, i, :], lg), "mx", n)
                for i in range(2):
                    n = 2 * s + i
                    need(e, "mx", n)
                    done(e.max_index(mi[:, i, :], mx[:, i, :], glo[:, i, 128:136]), "mi", n)
                need(e, "gx", s - 1)
                done(e.tensor_tensor(gd[:, :], mx[:, :, 1], mx[:, :, 0], ALU.subtract), "gd", s)
                need(e, "mi", 2 * s + 1)
                done(e.tensor_copy(mif[:, :, :], mi[:, :, 0:2]), "mif", s)
                need(e, "gx", s)
                done(e.tensor_scalar(gn[:, :], gx[:, :], 1.0, None, ALU.add), "gn", s)
                need(e, "gn", s)
                done(e.reciprocal(wsel[:, :, 0], gn[:, :]), "w0", s)
                need(e, "w0", s)
                done(e.tensor_tensor(wsel[:, :, 1], gx[:, :], wsel[:, :, 0], ALU.mult), "w1", s)
                need(e, "w1", s)
                need(e, "mif", s)
                for i in range(2):
                    n = 2 * s + i
                    done(e.tensor_scalar(t1[:, i, :], iota[:, :], mif[:, i, 0:1], wsel[:, i, 0:1],
                                         ALU.is_equal, ALU.mult), "ta", n)
                    done(e.tensor_scalar(t2[:, i, :], iota[:, :], mif[:, i, 1:2], wsel[:, i, 1:2],
                                         ALU.is_equal, ALU.mult), "tb", n)
                need(e, "tb", 2 * s + 1)
                done(e.tensor_tensor(wf[:, :, :], t1[:, :, :], t2[:, :, :], ALU.add), "wf", s)
                need(e, "wf", s)
                need(e, "wt", s - 1)
                for i in range(2):
                    n = 2 * s + i
                    done(e.scalar_tensor_tensor(
                        lw[:, i, :].rearrange("p (a r) -> p a r", r=16),
                        glo[:, i, 0:128].rearrange("p (a r) -> p a r", r=16), SCALING,
                        wf[:, i, :].unsqueeze(2).to_broadcast([P, 8, 16]), ALU.mult, ALU.mult), "lw", n)

            def v_fW(s):
                need(e, "wh", s)
                need(e, "fC", 2 * s - 1)
                done(e.tensor_tensor(LL[:, :], tb(("fW", s))[:, 0:256], LH[:, :].bitcast(F32), ALU.subtract),
                     "wl", s)

            def v_fC(n):
                t = n % NT
                need(e, "fC", n)
                need(e, "xb", n)
                done(e.tensor_tensor(X[:, t, :], gb(("fB", n))[:, :], X[:, t, :], ALU.add), "fx", n)

            done(e.memset(Sst[:, :, :].bitcast(F32), 0.0), "sinit", 0)
            done(e.memset(V[:, :, :, :, :], 0.0), "vz", 0)
            need(e, "vz", 0)
            done(e.memset(V[:, :, :, :, 16:17], 1.0), "vinit", 0)
            for item in prog:
                k, a = item[0], item[1:]
                if k == "W":
                    v_W(*a)
                elif k in ("aL", "fL"):
                    ln(k[0], *a)
                elif k in ("aT", "oT", "fT"):
                    front_l(k[0], *a)
                elif k == "aR":
                    v_aR(*a)
                elif k == "aH":
                    v_aH(*a)
                elif k == "aS":
                    v_aS(*a)
                elif k == "S":
                    v_S(*a)
                elif k == "PT":
                    v_PT(*a)
                elif k == "OT":
                    v_OT(*a)
                elif k == "oM":
                    v_oM(*a)
                elif k == "fG":
                    v_fG(*a)
                elif k == "fW":
                    v_fW(*a)
                elif k == "fC":
                    v_fC(*a)

        @block.gpsimd
        def _(e):
            done(e.memset(mh[:, :], -0.5), "mh", 0)
            need(e, "mh", 0)

            def power(c, s):
                w = 0 if c == "a" else 1
                need(e, "ne" + c, s)
                need(e, c + "xn", 2 * s - 1)
                done(e.tensor_tensor(rs[:, w, :], ve[:, w, :], mh[:, :], ALU.pow), "np" + c, s)

            def addbias(s):
                need(e, "c_bias", 0, 16)
                need(e, "fxn", 2 * s + 1)
                for i in range(2):
                    t = (2 * s + i) % NT
                    done(e.tensor_tensor(X[:, t, :], X[:, t, :], bias[:, :], ALU.add), "xb", 2 * s + i)

            for item in prog:
                if item[0] in ("aL", "fL"):
                    power(item[0][0], item[1])
                if item[0] == "fL":
                    addbias(item[1])


_IN = ["x", "wqa", "woa", "wqb", "wob", "wg", "wb", "wl", "bias", "trig", "iden", "idb", "mask", "iota"]


def kernel(L0_attn_a_x, L0_attn_a_w_qkv, L0_attn_a_w_o, L0_attn_b_wq, L0_attn_b_wk, L0_attn_b_wv,
           L0_attn_b_wo, L0_ffn_gate_w, L0_ffn_base_w, L0_ffn_base_b, L0_ffn_lora_A, L0_ffn_lora_B):
    import ml_dtypes
    import numpy as np
    import concourse.bacc as bacc
    from concourse.bass_utils import run_bass_kernel_spmd

    def lay(w):
        w = np.asarray(w)
        q = w[:, 0:512].reshape(512, 4, 2, 4, 8, 2).transpose(0, 5, 1, 3, 2, 4).reshape(512, 512)
        k = w[:, 512:640].reshape(512, 8, 8, 2).transpose(0, 3, 1, 2).reshape(512, 128)
        return np.ascontiguousarray(np.concatenate([q, k, w[:, 640:768]], axis=1))

    f = np.float32
    freq = f(1.0) / f(10000.0) ** (np.arange(0, 16, 2, dtype=f) / f(16))
    ang = np.arange(256, dtype=f)[:, None] * freq[None, :]
    c, s = np.cos(ang).astype(f), np.sin(ang).astype(f)
    trig = np.stack([c * f(0.25), s * f(0.25), c, s], axis=1).reshape(2, 128, 4, 8).transpose(1, 0, 2, 3)
    tri = np.where(np.arange(128)[None, :] > np.arange(128)[:, None], f(-1e30), f(0))
    arrays = {
        "x": np.ascontiguousarray(np.asarray(L0_attn_a_x).reshape(2048, 512)),
        "wqa": lay(L0_attn_a_w_qkv),
        "woa": np.ascontiguousarray(L0_attn_a_w_o),
        "wqb": lay(np.concatenate([np.asarray(L0_attn_b_wq), np.asarray(L0_attn_b_wk),
                                   np.asarray(L0_attn_b_wv)], axis=1)),
        "wob": np.ascontiguousarray(L0_attn_b_wo),
        "wg": np.ascontiguousarray(np.concatenate([np.asarray(L0_ffn_lora_A).reshape(128, 512).T,
                                                   np.asarray(L0_ffn_gate_w).T], axis=1)),
        "wb": np.ascontiguousarray(np.asarray(L0_ffn_base_w).T),
        "wl": np.ascontiguousarray(np.asarray(L0_ffn_lora_B).transpose(0, 2, 1).reshape(128, 512)),
        "bias": np.ascontiguousarray(np.broadcast_to(np.asarray(L0_ffn_base_b)[None, :], (128, 512))),
        "trig": np.ascontiguousarray(trig.reshape(128, 64)),
        "iden": np.eye(128, dtype=f),
        "idb": np.eye(128).astype(ml_dtypes.bfloat16),
        "mask": np.ascontiguousarray(np.tile(tri, (1, 4)).astype(ml_dtypes.bfloat16)),
        "iota": np.ascontiguousarray(np.broadcast_to(np.arange(8, dtype=f)[None, :], (128, 8))),
    }
    nc = bacc.Bacc("TRN2", target_bir_lowering=False, num_devices=1)
    args = [nc.dram_tensor("in_" + n, arrays[n].shape, mybir.dt.from_np(arrays[n].dtype),
                           kind="ExternalInput").ap() for n in _IN]
    out = nc.dram_tensor("out_0", (2048, 512), F32, kind="ExternalOutput").ap()
    hybrid_block_kernel(nc, *args, out)
    r = run_bass_kernel_spmd(nc, [{"in_" + n: a for n, a in arrays.items()}], core_ids=[0])
    return r.results[0]["out_0"].reshape(8, 256, 512)
```

```python
from contextlib import ExitStack

import concourse.bass as bass
from concourse import mybir

F32 = mybir.dt.float32
F32R = mybir.dt.float32r
U32 = mybir.dt.uint32
ALU = mybir.AluOpType
ACT = mybir.ActivationFunctionType
AX = mybir.AxisListType

P = 128
D = 512
NT = 16
NB = 8
NL = 2
SLOTS = NL * NB
EPS = 1e-5
SCALING = 2.0
LOWEST = -3e38

LAG_M, LAG_B, LAG_V, LAG_O = 7, 10, 18, 21
LATE = {"Wl": 0, "aV": 3, "fH": 2, "fV": 5, "xL": 0}
START = "aL0 aT0 aT1 aR0 aH0 aQ0 aK0 aQ1 aR1 aK1 aS0 aH1 aL1 aS1"
ORDER = ["AVMOB", "BVAMO", "ABMOV", "MBAOV", "OBMVA", "VOMAB", "BAVMO", "MVAOB", "OBAMV", "ABOVM", "OVMAB", "BVOAM",
         "ABMOV", "BAMVO", "MBVAO", "ABMVO", "ABMOV", "OABVM", "BMOVA", "ABMVO", "AVOMB", "ABOMV", "VBMAO", "OABMV"]
WAT = {
    0: [0, 0, 0, 0, 0, 1, 0, 1, 0, 1, 0, 1, 1, 0, 0, 0, 2, 0, 1, 1, 2, 1, 1, 0],
    6: [0, 0, 0, 0, 0, 0, 0, 0, 0, 0, 0, 0, 0, 0, 0, 0, 0, 0, 1, 1, 0, 1, 0, 1],
    9: [1, 1, 0, 0, 0, 0, 0, 0, 0, 1, 0, 0, 0, 1, 0, 0, 0, 0, 0, 0, 0, 0, 0, 0],
}
TABLE = [
    "fB0.0-2",
    "fA1.3-2 fG-2",
    "fB0.1-2",
    "fB0.2-2 fB1.0-2 fB1.1-2",
    "fB0.3-2 fB1.2-2",
    "fW-2",
    "fB1.3-2 aT0+1 fC0-2",
    "fC1-2 aT1+1 aQ0.0+1",
    "aK0.0+1",
    "aQ0.1+1",
    "",
    "aQ0.2+1 aK0.1+1 aQ0.3+1",
    "aK0.2+1 aR0+1 aK0.3+1",
    "aQ1.0+1 aH0+1",
    "aQ1.1+1",
    "aQ1.2+1 aQ1.3+1",
    "aK1.0+1 aR1+1",
    "aK1.1+1 aK1.2+1 aK1.3+1 aS0.0+1 oT0-1 aS0.1+1",
    "oT1-1 aS0.2+1 oM0.0-1",
    "aS0.3+1 oM1.0-1 aS0.4+1",
    "aH1+1 oM1.1-1",
    "oM0.1-1 oM1.2-1 oM0.2-1 oM0.3-1 oM1.3-1 aS1.0+1 fL-1 aS1.1+1",
    "aS1.2+1 aS1.3+1 aS1.4+1 fT0-1 fT1-1",
    "fA0.0-1 fA0.1-1 fA0.2-1 fA1.0-1 fA1.1-1 fA1.2-1 fA0.3-1 aL+2",
]

TRING = ("aT", "oT", "fT", "aS", "B", "M2", "OT", "fW")


def plan():
    def item(token, s):
        name, shift = token[:-2], int(token[-2:])
        k, s = name[:2], s + shift
        if not 0 <= s < SLOTS or (s == 0 and k[0] == "a") or token == "aL+2" and s == 1:
            return []
        n = 2 * s + int(name[2]) if len(name) > 2 else s
        return [(k, n, int(name[4])) if "." in name else (k, n)]

    count = {"aQ": 4, "aK": 4, "aS": 5}
    wk = iter(range(25))
    prog = [("W", next(wk)) for _ in range(4)]
    for x in START.split():
        k, n = x[:2], int(x[2:])
        prog += [(k, n, j) for j in range(count[k])] if k in count else [(k, n)]
    for c in range(24 * (SLOTS + 2)):
        s = c // 24
        if c % 6 == 0 and 0 < c <= 384:
            prog.append(("M1", c // 6 - 1))
        for name in ORDER[c % 24]:
            if name == "A" and c < 384:
                prog.append(("A", c // 3, c % 3))
            if name == "B" and 0 <= c - LAG_B < 384:
                prog.append(("B", (c - LAG_B) // 3, (c - LAG_B) % 3))
            if name in ("M", "O", "V"):
                lag = {"M": LAG_M, "O": LAG_O, "V": LAG_V}[name]
                if (c - lag) % 6 == 0 and 0 <= (c - lag) // 6 < 64:
                    prog.append(({"M": "M2", "O": "OT", "V": "PV"}[name], (c - lag) // 6))
        prog += [("W", next(wk)) for _ in range(WAT.get(s, [0] * 24)[c % 24])]
        for token in TABLE[c % 24].split():
            prog += item(token, s)
    return settle(prog)


def settle(prog):
    where = {it: i for i, it in enumerate(prog)}
    ring = [it for it in prog if it[0] in TRING]
    nth = {it: i for i, it in enumerate(ring)}
    banks = [it for it in prog if it[0] in ("aQ", "aK", "oM", "fA", "fB") and it[2] == 0]
    put = []
    for i, it in enumerate(prog):
        k, n = it[0], it[1]
        after = None
        if k in ("aT", "oT", "fT"):
            after, limit = ("xL", k[0], n), [({"a": "aQ", "o": "oM", "f": "fA"}[k[0]], n, 0)]
        elif k == "aR":
            after, limit = ("aV", n), [banks[j + 2] for j in [banks.index(("aK", n, 0))] if j + 2 < len(banks)]
        elif k == "aH":
            after, limit = ("aZ", n), [("aS", n, 0)] + ([("aR", n + 1)] if ("aR", n + 1) in where else [])
        elif k == "fG":
            after, limit = ("fH", n), [("fW", n)]
        elif k == "fW":
            after, limit = ("fV", n), [("fC", 2 * n)]
        elif k in ("aL", "fL"):
            after, limit = (k[0] + "N", n), [(k[0] + "T", 2 * n)]
        elif k == "W" and n > 3:
            after, limit = ("Wl", n), []
        if k == "W" and n <= 3:
            put.append((i, i, ("Wl", n)))
        if after is None:
            continue
        if k in TRING:
            j = nth[it] + 3
            limit += ring[j:j + 1]
        last = min([where[x] for x in limit] + [len(prog)]) - 1
        end, seen = i, 0
        while end < last and seen < LATE.get(after[0], 1):
            end += 1
            seen += prog[end][0] == "A"
            if end > i + 9 * LATE.get(after[0], 1):
                break
        put.append((end, i, after))
    put.sort()
    out = []
    for i, it in enumerate(prog):
        out.append(it)
        while put and put[0][0] == i:
            out.append(put.pop(0)[2])
    return out


def hybrid_block_kernel(nc, x_in, wqa, woa, wqb, wob, wg, wb, wl, bias_in, trig_in, iden_in,
                        mask_in, iota_in, out):
    prog = plan()

    tuse, guse, xuse = {}, {}, {}
    tfree, gfree, xfree = [], [], []
    for item in prog:
        k = item[0]
        if k in ("aT", "oT", "fT"):
            tuse[item] = len(tfree)
            tfree.append((k[0] + "l", item[1]))
            xuse[(k[0], item[1])] = len(xfree)
            xfree.append(({"a": "aK", "o": "oM", "f": "fB"}[k[0]], item[1]))
        elif k == "aS":
            tuse[item] = len(tfree)
            n, i = item[1:]
            tfree.append(("kt", n) if i == 0 else (("qa", 2 * n + (i - 2) // 2) if i % 2 == 0 else
                                                  ("qd", 2 * n + (i - 1) // 2)))
        elif k == "B":
            tuse[item] = len(tfree)
            tfree.append(("ex", 3 * item[1] + item[2]))
        elif k == "M2":
            tuse[item] = len(tfree)
            tfree.append(("mc", item[1]))
        elif k == "OT":
            tuse[item] = len(tfree)
            tfree.append(("on", item[1]))
        elif k == "fW":
            tuse[item] = len(tfree)
            tfree.append(("wl", item[1]))
        elif k in ("aQ", "aK", "oM", "fA", "fB") and item[2] == 0:
            guse[item[:2]] = len(gfree)
            gfree.append(({"aQ": "uq", "aK": "av", "oM": "ox", "fA": "fg", "fB": "fx"}[k], item[1]))

    with ExitStack() as ctx:
        def sb(name, shape, dt):
            return ctx.enter_context(nc.sbuf_tensor(name, shape, dt))

        def pb(name, shape):
            return ctx.enter_context(nc.psum_tensor(name, shape, F32))

        X = sb("X", [P, NT, D], F32)
        Wst = sb("Wst", [P, 2, 768], F32)
        WQh = sb("WQh", [P, 4, 768], F32R)
        WQl = sb("WQl", [P, 4, 768], F32R)
        WOh = sb("WOh", [P, 4, D], F32R)
        WOl = sb("WOl", [P, 4, D], F32R)
        WGh = sb("WGh", [P, 4, 136], F32R)
        WGl = sb("WGl", [P, 4, 136], F32R)
        WBh = sb("WBh", [P, 4, D], F32R)
        WBl = sb("WBl", [P, 4, D], F32R)
        WLh = sb("WLh", [P, D], F32R)
        WLl = sb("WLl", [P, D], F32R)
        xn = sb("xn", [P, 2, D], F32)
        at = sb("at", [P, 2, D], F32)
        XH = sb("XH", [P, 2, D], F32R)
        XL = sb("XL", [P, 2, D], F32R)
        U1 = sb("U1", [P, 2, 40, 8], F32)
        U2 = sb("U2", [P, 2, 40, 8], F32)
        Sst = sb("Sst", [P, 40, 64], F32R)
        QT = sb("QT", [P, 2, 4, 4, 2, 128], F32R)
        KT = sb("KT", [P, 2, 4, 256], F32R)
        V = sb("V", [P, 3, 2, 8, 32], F32)
        PTs = sb("PTs", [P, 3, 3, 512], F32)
        Os = sb("Os", [P, 512], F32)
        rc = sb("rc", [P, 16], F32)
        nm = sb("nm", [P, 2, 2, 4, 2], F32)
        mhl = sb("mhl", [P, 2, 2, 8], F32R)
        mT = sb("mT", [32, 128], F32)
        st6 = sb("st6", [P, 2, 2, 6], F32)
        mv = sb("mv", [P, 2, 2, 2], F32)
        ve = sb("ve", [P, 2, 2], F32)
        rs = sb("rs", [P, 2, 2], F32)
        half = sb("half", [P, 2], F32)
        glo = sb("glo", [P, 2, 136], F32)
        mx = sb("mx", [P, 2, 8], F32)
        mi = sb("mi", [P, 2, 8], U32)
        gd = sb("gd", [P, 2], F32)
        gx = sb("gx", [P, 2], F32)
        gn = sb("gn", [P, 2], F32)
        wsel = sb("wsel", [P, 2, 2], F32)
        mif = sb("mif", [P, 2, 2], F32)
        t1 = sb("t1", [P, 2, 8], F32)
        t2 = sb("t2", [P, 2, 8], F32)
        wf = sb("wf", [P, 2, 8], F32)
        LH = sb("LH", [P, 256], F32R)
        LL = sb("LL", [P, 256], F32R)
        bias = sb("bias", [P, D], F32)
        trig = sb("trig", [P, 2, 4, 8], F32)
        iden = sb("iden", [P, 128], F32)
        mask = sb("mask", [P, 256], F32)
        iota = sb("iota", [P, 8], F32)

        SA = [pb(f"SA{i}", [P, 512]) for i in range(2)]
        T = [pb(f"T{i}", [P, 512]) for i in range(3)]
        O = pb("O", [P, 512])
        G = [pb(f"G{i}", [P, 512]) for i in range(2)]

        sems, made, known = {}, {}, {}

        def sem(name):
            if name not in sems:
                sems[name] = ctx.enter_context(nc.semaphore("s_" + name))
            return sems[name]

        def done(ins, name, n):
            assert made.get(name, 0) == n, (name, n, made.get(name))
            made[name] = n + 1
            ins.then_inc(sem(name), 1)

        def need(e, name, n, step=1):
            v = step * (n + 1)
            if n >= 0 and known.get((id(e), name), 0) < v:
                known[(id(e), name)] = v
                e.wait_ge(sem(name), v)

        def tbank(e, item):
            k = tuse[item]
            if k >= 3:
                need(e, *tfree[k - 3])
            return T[k % 3]

        def tb(item):
            return T[tuse[item] % 3]

        def gbank(e, key):
            k = guse[key]
            if k >= 2:
                need(e, *gfree[k - 2])
            return G[k % 2]

        def gb(key):
            return G[guse[key] % 2]

        def cols(dram, c, n):
            return dram[c * P:(c + 1) * P, 0:n]

        wch = []
        for c in range(4):
            wch.append((cols(wqa, c, 768), WQh[:, c, :], WQl[:, c, :], 768))
        for c in range(4):
            wch.append((cols(woa, c, D), WOh[:, c, :], WOl[:, c, :], D))
        for c in range(4):
            wch.append((cols(wg, c, 136), WGh[:, c, :], WGl[:, c, :], 136))
        for c in range(4):
            wch.append((cols(wb, c, D), WBh[:, c, :], WBl[:, c, :], D))
        wch.append((cols(wl, 0, D), WLh[:, :], WLl[:, :], D))
        for c in range(4):
            wch.append((cols(wqb, c, 768), WQh[:, c, :], WQl[:, c, :], 768))
        for c in range(4):
            wch.append((cols(wob, c, D), WOh[:, c, :], WOl[:, c, :], D))
        wland = [PTs[:, k // 2, :, :].rearrange("p a b -> p (a b)")[:, (k % 2) * 768:(k % 2 + 1) * 768]
                 if k < 4 else Wst[:, k % 2, 0:wch[k][3]] for k in range(len(wch))]

        names = [it[1] for it in prog if it[0] == "W"]
        nw = len(wch)
        assert names[:nw] == list(range(nw))

        def wlanded(e, k):
            if k < 4:
                need(e, f"wf{k}", 0, 16)
            else:
                need(e, f"wd{k % 2}", (k - 4) // 2, 16)

        block = ctx.enter_context(nc.Block())

        @block.sync
        def _(e):
            def load(dst, src, name):
                e.dma_start(dst, src).then_inc(sem(name), 16)

            def xload(b):
                load(X[:, 2 * b:2 * b + 2, :],
                     x_in[256 * b:256 * b + 256, :].rearrange("(t p) d -> p t d", p=P), f"x{b}")

            xload(0)
            load(iden[:, :], iden_in, "c_id")
            load(wland[0], wch[0][0], "wf0")
            load(wland[1], wch[1][0], "wf1")
            load(trig[:, :, :, :].rearrange("p a b c -> p (a b c)"), trig_in, "c_trig")
            load(wland[2], wch[2][0], "wf2")
            load(wland[3], wch[3][0], "wf3")
            load(mask[:, :], mask_in, "c_mask")
            for b in range(1, NB):
                xload(b)
            load(bias[:, :], bias_in, "c_bias")
            load(iota[:, :], iota_in, "c_iota")
            for k in (4, 5):
                load(wland[k], wch[k][0], f"wd{k % 2}")
            ready = []

            def store():
                while ready:
                    n = ready.pop(0)
                    need(e, "fx", n)
                    e.dma_start(out[(n - NT) * P:(n - NT + 1) * P, :], X[:, n - NT, :]).then_inc(sem("out"), 16)

            for item in prog:
                if item[0] == "W" and 4 <= item[1] < nw - 2:
                    k = item[1] + 2
                    need(e, "wlo", k - 2)
                    load(wland[k], wch[k][0], f"wd{k % 2}")
                elif item[0] == "M2":
                    p = item[1]
                    s, gg = divmod(p, 4)
                    need(e, "mc", p)
                    if s >= 2:
                        need(e, "b", 3 * (8 * (s - 2) + 7) + 2)
                    for a in range(2):
                        dst = QT[64 * a + 48:64 * a + 50, s % 2, gg, :, :, :].rearrange("r j q t -> r (j q t)").bitcast(F32)
                        e.dma_start(dst, mT[16 * a:16 * a + 16, :]).then_inc(sem("md"), 16)
                    store()
                elif item[0] == "fC" and item[1] >= NT:
                    ready.append(item[1])
            store()
            e.wait_ge(sem("out"), 16 * NT)


        @block.tensor
        def _(e):
            def front(c, n):
                item = (c + "T", n)
                if c == "o":
                    need(e, "on", 4 * (n // 2) + 3)
                    src = at[:, n % 2, :]
                else:
                    need(e, c + "xn", n)
                    src = xn[:, n % 2, :]
                need(e, "c_id", 0, 16)
                t = tbank(e, item)
                for k in range(4):
                    ins = e.transpose(t[:, k * P:(k + 1) * P], src[:, k * P:(k + 1) * P], iden[:, :])
                done(ins, c + "t", n)

            def chunk(c, key, n, j, width, wh, wlo, more=False):
                bank = gbank(e, (key, n)) if j == 0 else gb((key, n))
                k = xuse[(c, n)] % 2
                need(e, c + "h", n)
                need(e, c + "l", n)
                xh = XH[:, k, j * P:(j + 1) * P]
                xl = XL[:, k, j * P:(j + 1) * P]
                o = bank[:, 0:width]
                e.matmul(o, xh, wh, start=(j == 0), stop=False, skip_group_check=True)
                e.matmul(o, xh, wlo, start=False, stop=False, skip_group_check=True)
                ins = e.matmul(o, xl, wh, start=False, stop=(j == 3 and not more), skip_group_check=True)
                if j == 3:
                    done(ins, key, n)

            def v_aQ(n, j):
                need(e, "wlo", 3 if n < 16 else 20)
                chunk("a", "aQ", n, j, 512, WQh[:, j, 0:512], WQl[:, j, 0:512])

            def v_aK(n, j):
                chunk("a", "aK", n, j, 256, WQh[:, j, 512:768], WQl[:, j, 512:768])

            def v_aS(n, i):
                t = tbank(e, ("aS", n, i))
                for name in ("hq1", "lq", "lk"):
                    need(e, name, n)
                for j in range(4):
                    h = 32 + 2 * j if i == 0 else (i - 1) * 8 + 2 * j
                    src = Sst[:, h:h + 2, :].rearrange("p a b -> p (a b)").bitcast(F32)
                    ins = e.transpose(t[:, j * P:(j + 1) * P], src, iden[:, :])
                done(ins, "st", 5 * n + i)

            def ones(s, gg):
                for n in (2 * s, 2 * s + 1):
                    need(e, "kt", n)
                    need(e, "qd" if gg % 2 == 0 else "qa", 2 * n + gg // 2)

            def v_A(u, i):
                s, g = divmod(u, 8)
                gg, r0 = g // 2, 64 * (g % 2)
                b, k = s % 2, 3 * u + i
                ones(s, gg)
                need(e, "m", k - 2)
                t = SA[k % 2]
                for j in range(4 if i == 0 else 2):
                    w = 128 if i == 0 else 256
                    h = j if i == 0 else 2 * (i - 1) + j
                    ins = e.matmul(t[:, j * w:(j + 1) * w], QT[r0:r0 + 48, b, gg, h, min(i, 1), :],
                                   KT[r0:r0 + 48, b, gg, 0:w], start=True, stop=True, skip_group_check=True)
                done(ins, "sa", k)

            def v_M2(p):
                need(e, "ml", p)
                t = tbank(e, ("M2", p))
                done(e.transpose(t[0:32, 0:128], mhl[:, :, :, :].rearrange("p a h b -> p (a h b)").bitcast(F32),
                                 iden[:, :]), "mt", p)

            def v_B(u, i):
                s, g = divmod(u, 8)
                gg, r0 = g // 2, 64 * (g % 2)
                b = s % 2
                need(e, "md", u // 2, 32)
                t = tbank(e, ("B", u, i))
                kt = 1 if i == 2 else 0
                done(e.matmul(t[:, :].rearrange("p (j q) -> p j q", j=4),
                              KT[r0:r0 + 50, b, gg, kt * P:(kt + 1) * P],
                              QT[r0:r0 + 50, b, gg, :, min(i, 1), :], start=True, stop=True,
                              skip_group_check=True), "b", 3 * u + i)

            def v_PV(p):
                s = p // 4
                need(e, "ex", 6 * p + 5)
                need(e, "sel", 4 * p + 3)
                need(e, "av", 2 * s + 1)
                need(e, "vinit", 0)
                need(e, "oc", p - 1)
                for u in (2 * p, 2 * p + 1):
                    g, q = u % 8, 64 * (u % 2)
                    e.matmul(O[q:q + 32, :], V[:, s % 3, 0, g, :], PTs[:, u % 3, 0, :],
                             start=True, stop=True, skip_group_check=True)
                    e.matmul(O[q + 32:q + 64, :], V[:, s % 3, 0, g, :], PTs[:, u % 3, 1, :],
                             start=True, stop=False, skip_group_check=True)
                for u in (2 * p, 2 * p + 1):
                    g, q = u % 8, 64 * (u % 2)
                    ins = e.matmul(O[q + 32:q + 64, :], V[:, s % 3, 1, g, :], PTs[:, u % 3, 2, :],
                                   start=False, stop=True, skip_group_check=True)
                done(ins, "pv", p)

            def v_OT(p):
                need(e, "oc", p)
                t = tbank(e, ("OT", p))
                for j in range(4):
                    ins = e.transpose(t[:, j * P:(j + 1) * P], Os[:, j * P:(j + 1) * P], iden[:, :])
                done(ins, "oT", p)

            def v_oM(n, j):
                need(e, "wlo", 7 if n < 16 else 24)
                chunk("o", "oM", n, j, 512, WOh[:, j, :], WOl[:, j, :])

            def v_fA(n, j):
                need(e, "wlo", 11)
                chunk("f", "fA", n, j, 136, WGh[:, j, :], WGl[:, j, :])

            def v_fB(n, j):
                need(e, "wlo", 15)
                chunk("f", "fB", n, j, 512, WBh[:, j, :], WBl[:, j, :], more=True)

            def v_fW(s):
                t = tbank(e, ("fW", s))
                for i in range(2):
                    need(e, "lw", 2 * s + i)
                    ins = e.transpose(t[:, i * P:(i + 1) * P], glo[:, i, 0:128], iden[:, :])
                done(ins, "wt", s)

            def v_fC(n):
                need(e, "wlo", 16)
                need(e, "wh", n // 2)
                need(e, "wl", n // 2)
                g = gb(("fB", n))
                i = n % 2
                e.matmul(g[:, :], LH[:, i * P:(i + 1) * P], WLh[:, :], start=False, stop=False,
                         skip_group_check=True)
                e.matmul(g[:, :], LH[:, i * P:(i + 1) * P], WLl[:, :], start=False, stop=False,
                         skip_group_check=True)
                done(e.matmul(g[:, :], LL[:, i * P:(i + 1) * P], WLh[:, :], start=False, stop=True,
                              skip_group_check=True), "fC", n)

            for item in prog:
                k, a = item[0], item[1:]
                if k in ("aT", "oT", "fT"):
                    front(k[0], *a)
                elif k == "aQ":
                    v_aQ(*a)
                elif k == "aK":
                    v_aK(*a)
                elif k == "aS":
                    v_aS(*a)
                elif k == "A":
                    v_A(*a)
                elif k == "M2":
                    v_M2(*a)
                elif k == "B":
                    v_B(*a)
                elif k == "PV":
                    v_PV(*a)
                elif k == "OT":
                    v_OT(*a)
                elif k == "oM":
                    v_oM(*a)
                elif k == "fA":
                    v_fA(*a)
                elif k == "fB":
                    v_fB(*a)
                elif k == "fW":
                    v_fW(*a)
                elif k == "fC":
                    v_fC(*a)

        @block.scalar
        def _(e):
            def copy(dst, src):
                return e.activation(dst, src, ACT.Copy)

            def front_h(c, n):
                k = xuse[(c, n)]
                need(e, c + "t", n)
                if k >= 2:
                    need(e, *xfree[k - 2])
                done(copy(XH[:, k % 2, :], tb((c + "T", n))[:, :]), c + "h", n)

            def s_W(k):
                wlanded(e, k)
                if 17 <= k < 21:
                    need(e, "aK", 15)
                if 21 <= k:
                    need(e, "oM", 15)
                n = wch[k][3]
                done(copy(wch[k][1], wland[k]), "whi", k)

            def s_aV(n):
                need(e, "uk", n)
                s = n // 2
                if s >= 3:
                    need(e, "pv", 4 * (s - 3) + 3)
                need(e, "vinit", 0)
                done(copy(V[:, s % 3, n % 2, :, 0:16],
                          gb(("aK", n))[:, 128:256].rearrange("p (g d) -> p g d", d=16)), "av", n)

            def s_aH(n):
                need(e, "ro", n)
                need(e, "st", 5 * (n - 1) + 4)
                need(e, "sinit", 0)
                for r in range(2):
                    done(copy(Sst[:, 0:32, 32 * r:32 * r + 16].rearrange("p a (h f) -> p h a f", h=2),
                              U1[:, :, 0:32, :]), f"hq{r}", n)
                for r in range(2):
                    done(copy(Sst[:, 32:40, 16 * r:16 * r + 16].rearrange("p a (h f) -> p h a f", h=2),
                              U1[:, :, 32:40, :]), f"hk{r}", n)

            def s_aS(n, i):
                if i in (0, 2, 4):
                    t = tb(("aS", n, i))
                    s, q = divmod(n, 2)
                    need(e, "st", 5 * n + i)
                    if i == 0:
                        if s >= 2:
                            need(e, "b", 3 * (8 * (s - 2) + 7) + 2)
                        done(copy(KT[:, s % 2, :, q * P:(q + 1) * P],
                                  t[:, :].rearrange("p (g k) -> p g k", g=4)), "kt", n)
                    else:
                        if s >= 2:
                            need(e, "b", 3 * (8 * (s - 2) + 7) + 2)
                        done(copy(QT[:, s % 2, i - 1, :, q, :],
                                  t[:, :].rearrange("p (g k) -> p g k", g=4)), "qa", 2 * n + (i - 2) // 2)

            def s_M2(p):
                need(e, "mt", p)
                need(e, "md", p - 1, 32)
                done(copy(mT[:, :], tb(("M2", p))[0:32, 0:128]), "mc", p)

            def s_B(u, i):
                need(e, "b", 3 * u + i)
                if u >= 3:
                    need(e, "pv", (u - 3) // 2)
                else:
                    need(e, "wlo", 3)
                done(e.activation(PTs[:, u % 3, i, :], tb(("B", u, i))[:, :], ACT.Exp), "ex", 3 * u + i)

            def s_PV(p):
                need(e, "pv", p)
                need(e, "oT", p - 1)
                done(copy(Os[:, :], O[:, :]), "oc", p)

            def s_fA(n, j):
                if j < 3:
                    return
                need(e, "fA", n)
                need(e, "wt", n // 2 - 1)
                done(copy(glo[:, n % 2, :], gb(("fA", n))[:, 0:136]), "fg", n)

            def s_fG(s):
                need(e, "gd", s)
                done(e.activation(gx[:, :], gd[:, :], ACT.Exp), "gx", s)

            def s_fW(s):
                need(e, "wt", s)
                need(e, "fC", 2 * s - 1)
                done(copy(LH[:, :], tb(("fW", s))[:, 0:256]), "wh", s)

            for item in prog:
                k, a = item[0], item[1:]
                if k == "W":
                    s_W(*a)
                elif k in ("aT", "oT", "fT"):
                    front_h(k[0], *a)
                elif k == "aV":
                    s_aV(*a)
                elif k == "aH":
                    s_aH(*a)
                elif k == "aS":
                    s_aS(*a)
                elif k == "M2":
                    s_M2(*a)
                elif k == "B":
                    s_B(*a)
                elif k == "PV":
                    s_PV(*a)
                elif k == "fA":
                    s_fA(*a)
                elif k == "fG":
                    s_fG(*a)
                elif k == "fW":
                    s_fW(*a)

        @block.vector
        def _(e):
            def front_l(c, n):
                k = xuse[(c, n)]
                need(e, c + "h", n)
                if k >= 2:
                    need(e, *xfree[k - 2])
                done(e.tensor_tensor(XL[:, k % 2, :], tb((c + "T", n))[:, :], XH[:, k % 2, :].bitcast(F32),
                                     ALU.subtract), c + "l", n)

            def v_W(k):
                need(e, "whi", k)
                if 17 <= k < 21:
                    need(e, "aK", 15)
                if 21 <= k:
                    need(e, "oM", 15)
                done(e.tensor_tensor(wch[k][2], wland[k], wch[k][1].bitcast(F32), ALU.subtract), "wlo", k)

            def stats(c, s):
                w = 0 if c == "a" else 1
                if c == "a":
                    if s < NB:
                        need(e, f"x{s}", 0, 16)
                    else:
                        need(e, "fx", 2 * (s - NB) + 1)
                else:
                    need(e, "ox", 2 * s + 1)
                for i in range(2):
                    t = (2 * s + i) % NT
                    done(e.bn_stats(st6[:, w, i, :], X[:, t, :]), "nb" + c, 2 * s + i)
                for i in range(2):
                    need(e, "nb" + c, 2 * s + i)
                    done(e.bn_aggr(mv[:, w, i, :], st6[:, w, i, :]), "ng" + c, 2 * s + i)
                need(e, "ng" + c, 2 * s + 1)
                need(e, "np" + c, s - 1)
                done(e.tensor_scalar(ve[:, w, :], mv[:, w, :, 1], EPS, None, ALU.add), "ne" + c, s)

            def norm(c, s):
                w = 0 if c == "a" else 1
                need(e, "np" + c, s)
                for i in range(2):
                    n = 2 * s + i
                    t = n % NT
                    need(e, lnfree[(c, s)][0], lnfree[(c, s)][1] + i)
                    done(e.tensor_scalar(xn[:, i, :], X[:, t, :], mv[:, w, i, 0:1], rs[:, w, i:i + 1],
                                         ALU.subtract, ALU.mult), c + "xn", n)

            lnfree, last = {}, None
            for it in prog:
                if it[0] in ("aN", "fN"):
                    lnfree[(it[0][0], it[1])] = (last[0] + "t", 2 * last[1]) if last else ("at", -2)
                    last = (it[0][0], it[1])

            def v_aR(n):
                q = n % 2
                need(e, "c_trig", 0, 16)
                need(e, "aQ", n)
                need(e, "hk1", n - 1)
                need(e, "lk", n - 1)
                g = gb(("aQ", n))[:, :].rearrange("p (h a f) -> p h a f", h=2, f=8)

                def tr(i, h):
                    return trig[:, q, i, :].unsqueeze(1).unsqueeze(1).to_broadcast([P, 2, h, 8])

                e.tensor_tensor(U1[:, :, 0:32, :], g, tr(0, 32), ALU.mult)
                done(e.tensor_tensor(U2[:, :, 0:32, :], g, tr(1, 32), ALU.mult), "uq", n)
                need(e, "aK", n)
                g = gb(("aK", n))[:, 0:128].rearrange("p (h a f) -> p h a f", h=2, f=8)
                e.tensor_tensor(U1[:, :, 32:40, :], g, tr(2, 8), ALU.mult)
                done(e.tensor_tensor(U2[:, :, 32:40, :], g, tr(3, 8), ALU.mult), "uk", n)
                need(e, "uk", n)
                e.tensor_tensor(U1[:, 0, :, :], U1[:, 0, :, :], U2[:, 1, :, :], ALU.subtract)
                done(e.tensor_tensor(U1[:, 1, :, :], U1[:, 1, :, :], U2[:, 0, :, :], ALU.add), "ro", n)

            def v_aZ(n):
                need(e, "ro", n)
                need(e, "hq0", n)
                done(e.tensor_tensor(Sst[:, 0:32, 16:32].rearrange("p a (h f) -> p h a f", h=2),
                                     U1[:, :, 0:32, :],
                                     Sst[:, 0:32, 0:16].rearrange("p a (h f) -> p h a f", h=2).bitcast(F32),
                                     ALU.subtract), "lq", n)
                need(e, "hk0", n)
                need(e, "hk1", n)
                done(e.tensor_tensor(Sst[:, 32:40, 32:48].rearrange("p a (h f) -> p h a f", h=2),
                                     U1[:, :, 32:40, :],
                                     Sst[:, 32:40, 0:16].rearrange("p a (h f) -> p h a f", h=2).bitcast(F32),
                                     ALU.subtract), "lk", n)
                need(e, "lq", n)
                need(e, "lk", n)

            def v_aS(n, i):
                if i in (1, 3):
                    t = tb(("aS", n, i))
                    s, q = divmod(n, 2)
                    need(e, "st", 5 * n + i)
                    if s >= 2:
                        need(e, "b", 3 * (8 * (s - 2) + 7) + 2)
                    done(e.tensor_copy(QT[:, s % 2, i - 1, :, q, :],
                                       t[:, :].rearrange("p (g k) -> p g k", g=4)), "qd", 2 * n + (i - 1) // 2)

            def v_A(u, i):
                p, k = u // 2, 3 * u + i
                need(e, "sa", k)
                if i == 0:
                    need(e, "ml", p - 2)
                need(e, "c_mask", 0, 16)
                w = 128 if i == 0 else 256
                for j in range(512 // w):
                    h = j if i == 0 else 2 * (i - 1) + j
                    x = SA[k % 2][:, j * w:(j + 1) * w]
                    ins = e.tensor_tensor_reduce(x, x, mask[:, 256 - w:256], 1.0, LOWEST, ALU.add, ALU.max,
                                                 nm[:, p % 2, u % 2, h, min(i, 1):min(i, 1) + 1])
                done(ins, "m", k)

            def v_M1(p):
                src = nm[:, p % 2, :, :, :].rearrange("p a j q -> p a (j q)")
                need(e, "m", 6 * p + 5)
                need(e, "mt", p - 1)
                done(e.tensor_copy(mhl[:, :, 0, :], src), "mh", p)
                need(e, "mh", p)
                done(e.tensor_tensor(mhl[:, :, 1, :], src, mhl[:, :, 0, :].bitcast(F32), ALU.subtract), "ml", p)

            def v_OT(p):
                s, gg = divmod(p, 4)
                need(e, "oT", p)
                need(e, "ot", 2 * s - 1)
                t = tb(("OT", p))[:, :].rearrange("p (j a q d) -> p j a q d", j=4, a=2, q=2)
                need(e, "on", p - 1)
                done(e.reciprocal(rc[:, :].rearrange("p (j a q) -> p j a q", j=4, a=2), t[:, :, :, :, 16]),
                     "rc", p)
                need(e, "rc", p)
                for q in range(2):
                    dst = at[:, q, gg * 128:(gg + 1) * 128].rearrange("p (a j d) -> p j a d", a=2, j=4)
                    rb = rc[:, :].rearrange("p (j a q) -> p j a q", j=4, a=2)[:, :, :, q]
                    ins = e.tensor_tensor(dst, t[:, :, :, q, 0:16],
                                          rb.unsqueeze(3).to_broadcast([P, 4, 2, 16]), ALU.mult)
                done(ins, "on", p)

            def v_oM(n, j):
                if j < 3:
                    return
                t = n % NT
                need(e, "oM", n)
                done(e.tensor_tensor(X[:, t, :], gb(("oM", n))[:, :], X[:, t, :], ALU.add), "ox", n)

            def v_fG(s):
                need(e, "c_iota", 0, 16)
                for i in range(2):
                    n = 2 * s + i
                    need(e, "fg", n)
                    lg = glo[:, i, 128:136]
                    done(e.max(mx[:, i, :], lg), "mx", n)
                for i in range(2):
                    n = 2 * s + i
                    need(e, "mx", n)
                    done(e.max_index(mi[:, i, :], mx[:, i, :], glo[:, i, 128:136]), "mi", n)
                need(e, "gx", s - 1)
                done(e.tensor_tensor(gd[:, :], mx[:, :, 1], mx[:, :, 0], ALU.subtract), "gd", s)
                need(e, "mi", 2 * s + 1)
                done(e.tensor_copy(mif[:, :, :], mi[:, :, 0:2]), "mif", s)

            def v_fH(s):
                need(e, "gx", s)
                done(e.tensor_scalar(gn[:, :], gx[:, :], 1.0, None, ALU.add), "gn", s)
                need(e, "gn", s)
                done(e.reciprocal(wsel[:, :, 0], gn[:, :]), "w0", s)
                need(e, "w0", s)
                done(e.tensor_tensor(wsel[:, :, 1], gx[:, :], wsel[:, :, 0], ALU.mult), "w1", s)
                need(e, "w1", s)
                need(e, "mif", s)
                for i in range(2):
                    n = 2 * s + i
                    done(e.tensor_scalar(t1[:, i, :], iota[:, :], mif[:, i, 0:1], wsel[:, i, 0:1],
                                         ALU.is_equal, ALU.mult), "ta", n)
                    done(e.tensor_scalar(t2[:, i, :], iota[:, :], mif[:, i, 1:2], wsel[:, i, 1:2],
                                         ALU.is_equal, ALU.mult), "tb", n)
                need(e, "tb", 2 * s + 1)
                done(e.tensor_tensor(wf[:, :, :], t1[:, :, :], t2[:, :, :], ALU.add), "wf", s)
                need(e, "wf", s)
                need(e, "wt", s - 1)
                for i in range(2):
                    n = 2 * s + i
                    done(e.scalar_tensor_tensor(
                        glo[:, i, 0:128].rearrange("p (a r) -> p a r", r=16),
                        glo[:, i, 0:128].rearrange("p (a r) -> p a r", r=16), SCALING,
                        wf[:, i, :].unsqueeze(2).to_broadcast([P, 8, 16]), ALU.mult, ALU.mult), "lw", n)

            def v_fW(s):
                need(e, "wh", s)
                need(e, "fC", 2 * s - 1)
                done(e.tensor_tensor(LL[:, :], tb(("fW", s))[:, 0:256], LH[:, :].bitcast(F32), ALU.subtract),
                     "wl", s)

            def v_fC(n):
                t = n % NT
                need(e, "fC", n)
                need(e, "xb", n)
                done(e.tensor_tensor(X[:, t, :], gb(("fB", n))[:, :], X[:, t, :], ALU.add), "fx", n)

            done(e.memset(Sst[:, :, :].bitcast(F32), 0.0), "sz", 0)
            need(e, "sz", 0)
            done(e.memset(Sst[:, 32:40, 48:50].bitcast(F32), -1.0), "sinit", 0)
            done(e.memset(V[:, :, :, :, :], 0.0), "vz", 0)
            need(e, "vz", 0)
            done(e.memset(V[:, :, :, :, 16:17], 1.0), "vinit", 0)
            for item in prog:
                k, a = item[0], item[1:]
                if k == "Wl":
                    v_W(*a)
                elif k in ("aL", "fL"):
                    stats(k[0], *a)
                elif k in ("aN", "fN"):
                    norm(k[0], *a)
                elif k == "xL":
                    front_l(*a)
                elif k == "aR":
                    v_aR(*a)
                elif k == "aZ":
                    v_aZ(*a)
                elif k == "aS":
                    v_aS(*a)
                elif k == "A":
                    v_A(*a)
                elif k == "M1":
                    v_M1(*a)
                elif k == "OT":
                    v_OT(*a)
                elif k == "oM":
                    v_oM(*a)
                elif k == "fG":
                    v_fG(*a)
                elif k == "fH":
                    v_fH(*a)
                elif k == "fV":
                    v_fW(*a)
                elif k == "fC":
                    v_fC(*a)

        @block.gpsimd
        def _(e):
            done(e.memset(half[:, :], -0.5), "half", 0)
            need(e, "half", 0)

            def power(c, s):
                w = 0 if c == "a" else 1
                need(e, "ne" + c, s)
                need(e, c + "xn", 2 * s - 1)
                done(e.tensor_tensor(rs[:, w, :], ve[:, w, :], half[:, :], ALU.pow), "np" + c, s)

            def addbias(s):
                need(e, "c_bias", 0, 16)
                need(e, "fxn", 2 * s + 1)
                for i in range(2):
                    t = (2 * s + i) % NT
                    done(e.tensor_tensor(X[:, t, :], X[:, t, :], bias[:, :], ALU.add), "xb", 2 * s + i)

            def causal(u, i):
                blk = PTs[:, u % 3, i, :].rearrange("p (j q) -> p j q", j=4)
                need(e, "ex", 3 * u + i)
                done(e.affine_select(out=blk, in_=blk, compare_op=ALU.is_ge, fill=0.0, base=0,
                                     pattern=[[0, 4], [1, 128]], channel_multiplier=-1), "sel", 2 * u + i // 2)

            for item in prog:
                if item[0] == "B" and item[2] != 1:
                    causal(*item[1:])
                if item[0] in ("aL", "fL"):
                    power(item[0][0], item[1])
                if item[0] == "fN":
                    addbias(item[1])


_IN = ["x", "wqa", "woa", "wqb", "wob", "wg", "wb", "wl", "bias", "trig", "iden", "mask", "iota"]


def kernel(L0_attn_a_x, L0_attn_a_w_qkv, L0_attn_a_w_o, L0_attn_b_wq, L0_attn_b_wk, L0_attn_b_wv,
           L0_attn_b_wo, L0_ffn_gate_w, L0_ffn_base_w, L0_ffn_base_b, L0_ffn_lora_A, L0_ffn_lora_B):
    import numpy as np
    import concourse.bacc as bacc
    from concourse.bass_utils import run_bass_kernel_spmd

    def lay(w):
        w = np.asarray(w)
        q = w[:, 0:512].reshape(512, 4, 2, 4, 8, 2).transpose(0, 5, 1, 3, 2, 4).reshape(512, 512)
        k = w[:, 512:640].reshape(512, 8, 8, 2).transpose(0, 3, 1, 2).reshape(512, 128)
        return np.ascontiguousarray(np.concatenate([q, k, w[:, 640:768]], axis=1))

    f = np.float32
    freq = f(1.0) / f(10000.0) ** (np.arange(0, 16, 2, dtype=f) / f(16))
    ang = np.arange(256, dtype=f)[:, None] * freq[None, :]
    c, s = np.cos(ang).astype(f), np.sin(ang).astype(f)
    trig = np.stack([c * f(0.25), s * f(0.25), c, s], axis=1).reshape(2, 128, 4, 8).transpose(1, 0, 2, 3)
    tri = np.where(np.arange(128)[None, :] > np.arange(128)[:, None], f(-1e30), f(0))
    arrays = {
        "x": np.ascontiguousarray(np.asarray(L0_attn_a_x).reshape(2048, 512)),
        "wqa": lay(L0_attn_a_w_qkv),
        "woa": np.ascontiguousarray(L0_attn_a_w_o),
        "wqb": lay(np.concatenate([np.asarray(L0_attn_b_wq), np.asarray(L0_attn_b_wk),
                                   np.asarray(L0_attn_b_wv)], axis=1)),
        "wob": np.ascontiguousarray(L0_attn_b_wo),
        "wg": np.ascontiguousarray(np.concatenate([np.asarray(L0_ffn_lora_A).reshape(128, 512).T,
                                                   np.asarray(L0_ffn_gate_w).T], axis=1)),
        "wb": np.ascontiguousarray(np.asarray(L0_ffn_base_w).T),
        "wl": np.ascontiguousarray(np.asarray(L0_ffn_lora_B).transpose(0, 2, 1).reshape(128, 512)),
        "bias": np.ascontiguousarray(np.broadcast_to(np.asarray(L0_ffn_base_b)[None, :], (128, 512))),
        "trig": np.ascontiguousarray(trig.reshape(128, 64)),
        "iden": np.eye(128, dtype=f),
        "mask": np.ascontiguousarray(np.concatenate([np.zeros((128, 128), f), tri], axis=1)),
        "iota": np.ascontiguousarray(np.broadcast_to(np.arange(8, dtype=f)[None, :], (128, 8))),
    }
    nc = bacc.Bacc("TRN2", target_bir_lowering=False, num_devices=1)
    args = [nc.dram_tensor("in_" + n, arrays[n].shape, mybir.dt.from_np(arrays[n].dtype),
                           kind="ExternalInput").ap() for n in _IN]
    out = nc.dram_tensor("out_0", (2048, 512), F32, kind="ExternalOutput").ap()
    hybrid_block_kernel(nc, *args, out)
    r = run_bass_kernel_spmd(nc, [{"in_" + n: a for n, a in arrays.items()}], core_ids=[0])
    return r.results[0]["out_0"].reshape(8, 256, 512)
```

```python
from contextlib import ExitStack

import concourse.bass as bass
from concourse import mybir

F32 = mybir.dt.float32
F32R = mybir.dt.float32r
U32 = mybir.dt.uint32
ALU = mybir.AluOpType
ACT = mybir.ActivationFunctionType
AX = mybir.AxisListType

P = 128
D = 512
NT = 16
NB = 8
NL = 2
SLOTS = NL * NB
EPS = 1e-5
SCALING = 2.0
LOWEST = -3e38

LAG_M, LAG_B, LAG_V, LAG_O = 7, 11, 18, 21
LATE = {"Wl": 0, "aN": 2, "aO": 0, "aV": 2, "aZ": 0, "fH": 2, "fN": 2, "xL": 0}
HEAD = """
aL0 aL1 aT0 aT1 aK0.0 W aQ0.0 aQ0.1 aK0.1 aQ0.2 aQ0.3 aK0.2 aK0.3 W aQ1.0 W aQ1.1 aQ1.2 aK1.0 aQ1.3 W aK1.1 aR0
aK1.2 aH0 aR1 aS0.0 aK1.3 aS0.1 aS0.2 aS0.3 aS0.4 aH1 aS1.0 aL2 aS1.1 aL3 aT2 A0.0 A0.1 aS1.2 W aS1.3 W aS1.4
A0.2 A1.0 A1.1 A1.2 A2.0 aQ2.0 aK2.0 M10 M20 A2.1 W A2.2 aT3 A3.0 W A3.1 W aQ2.1 B0.0 A3.2 B0.1 M11 W B0.2 A4.0
aK2.1 A4.1 aQ2.2 aK2.2 aQ2.3 B1.0 aR2 M21 aK2.3 B1.1 B1.2 A4.2 A5.0 aQ3.0 aQ3.1 A5.1 W aQ3.2 B2.0 A5.2 aH2 W M12
M22 aK3.0 PV0 aQ3.3 aS2.0 aK3.1 aR3 aK3.2 aK3.3 B2.1 aS2.1 A6.0 A6.1 B2.2 W B3.0 aS2.2 B3.1 W A6.2 OT0 aS2.3
aS2.4 aL4 A7.0 aH3 A7.1 B3.2 W aS3.0 aS3.1 B4.0 W A7.2 aS3.2 aL5 aS3.3 aS3.4 W"""
TAIL = """
PV61 fA29.1 fB28.0 B124.1 M163 OT61 fA29.2 fA29.3 M263 B124.2 fG14 fB28.1 fB29.0 B125.0 fB28.2 B125.1 B125.2
fB29.1 B126.0 B126.1 fB29.2 fB28.3 fW14 B126.2 PV62 B127.0 B127.1 fC28 B127.2 OT62 fB29.3 PV63 fC29 OT63 oT30
oT31 oM30.0 oM30.1 oM31.0 oM30.2 oM31.1 oM30.3 oM31.2 fL30 oM31.3 fL31 fT30 fT31 fA30.0 fA30.1 fA30.2 fA31.0
fA30.3 fA31.1 fA31.2 fA31.3 fB31.0 fB30.0 fB30.1 fG15 fB30.2 fB31.1 fB30.3 fW15 fB31.2 fB31.3 fC30 fC31"""
ORDER = ["VMAOB", "BMAVO", "ABVOM", "MBAVO", "BOMVA", "OVMAB", "BAMOV", "OVBMA", "OBVMA", "ABOVM", "BAMOV", "OMABV",
         "AOBMV", "BAMVO", "MVBOA", "AVMBO", "AMBOV", "VBAOM", "VMBOA", "ABMOV", "MVOAB", "OBAMV", "VBOAM", "AOBMV"]
WAT = {
    6: [0, 0, 0, 0, 0, 0, 0, 0, 0, 0, 0, 0, 0, 0, 0, 0, 0, 1, 0, 0, 1, 0, 1, 1],
    9: [1, 1, 0, 1, 0, 0, 0, 0, 0, 0, 0, 0, 0, 0, 0, 0, 0, 0, 0, 1, 0, 0, 0, 0],
}
TABLE = [
    "",
    "fA1.1-2 fB0.0-2 fA1.2-2 fA1.3-2 fG-2",
    "",
    "fB0.1-2 fB0.2-2 fB1.0-2",
    "fB0.3-2 fB1.1-2 fB1.2-2 fW-2",
    "",
    "aT0+1 fC0-2 fB1.3-2",
    "fC1-2",
    "aQ0.0+1",
    "aT1+1 aQ0.1+1",
    "",
    "aQ0.2+1 aQ0.3+1",
    "aK0.0+1 aK0.1+1 aK0.2+1 aR0+1 aK0.3+1",
    "",
    "aQ1.0+1",
    "aH0+1 aQ1.1+1 aQ1.2+1",
    "aK1.0+1 oT0-1 aQ1.3+1",
    "aR1+1 aK1.1+1 aK1.2+1 aK1.3+1 aS0.0+1",
    "oT1-1 aS0.1+1 aS0.2+1 oM0.0-1",
    "oM0.1-1",
    "oM1.0-1 aS0.3+1",
    "aH1+1 aS0.4+1 oM1.1-1 aL0+2",
    "oM1.2-1 oM0.2-1 oM0.3-1 oM1.3-1 aS1.0+1 fL0-1 fL1-1 aS1.1+1 aS1.2+1 aS1.3+1 fT0-1 fT1-1 aS1.4+1 fA0.0-1 fA0.1-1 fA0.2-1 fA0.3-1 aL1+2 fA1.0-1",
    "",
]

TRING = ("aT", "oT", "fT", "aS", "B", "M2", "OT", "fW")


def plan():
    def item(token, s):
        name, shift = token[:-2], int(token[-2:])
        k, s = name[:2], s + shift
        if not 0 <= s < SLOTS:
            return []
        n = 2 * s + int(name[2]) if len(name) > 2 else s
        return [(k, n, int(name[4])) if "." in name else (k, n)]

    wk = iter(range(25))

    def listed(text):
        out = []
        for x in text.split():
            if x == "W":
                out.append(("W", next(wk)))
            else:
                k = 1 if x[0] in "AB" else 2
                out.append((x[:k], *[int(y) for y in x[k:].split(".")]))
        return out

    prog = listed(HEAD)
    for c in range(24, 24 * SLOTS):
        s = c // 24
        if c % 6 == 0:
            prog.append(("M1", c // 6 - 1))
        for name in ORDER[c % 24]:
            if name == "A":
                prog.append(("A", c // 3, c % 3))
            if name == "B":
                prog.append(("B", (c - LAG_B) // 3, (c - LAG_B) % 3))
            if name in ("M", "O", "V"):
                lag = {"M": LAG_M, "O": LAG_O, "V": LAG_V}[name]
                if (c - lag) % 6 == 0:
                    prog.append(({"M": "M2", "O": "OT", "V": "PV"}[name], (c - lag) // 6))
        prog += [("W", next(wk)) for _ in range(WAT.get(s, [0] * 24)[c % 24])]
        for token in TABLE[c % 24].split():
            prog += item(token, s)
    prog += listed(TAIL)
    return settle(prog)


def follow(prog, i, last, late):
    end, seen = i, 0
    while end < min(last, i + 9 * late) and seen < late:
        end += 1
        seen += prog[end][0] == "A"
    return end


def settle(prog):
    where = {it: i for i, it in enumerate(prog)}
    ring = [it for it in prog if it[0] in TRING]
    nth = {it: i for i, it in enumerate(ring)}
    banks = [it for it in prog if it[0] in ("aQ", "aK", "oM", "fA", "fB") and it[2] == 0]
    put = []
    for i, it in enumerate(prog):
        k, n = it[0], it[1]
        after = None
        if k in ("aT", "oT", "fT"):
            after, limit = ("xL", k[0], n), [({"a": "aQ", "o": "oM", "f": "fA"}[k[0]], n, 0)]
        elif k == "aR":
            j = banks.index(("aK", n, 0))
            after, limit = ("aV", n), banks[j + 2:j + 3]
        elif k == "aH":
            after, limit = ("aZ", n), [("aS", n, 0)] + ([("aR", n + 1)] if ("aR", n + 1) in where else [])
        elif k == "fA" and it[2] == 3:
            j = banks.index(("fA", n, 0))
            after, limit = ("fE", n), [("fG", n // 2)] + banks[j + 2:j + 3]
        elif k == "fG":
            after, limit = ("fH", n), [("fW", n)]
        elif k == "fW":
            after, limit = ("fV", n), [("fC", 2 * n)]
        elif k in ("aL", "fL"):
            after, limit = (k[0] + "N", n), [(k[0] + "T", n)]
        elif k == "W" and n > 3:
            after, limit = ("Wl", n), []
        if k == "W" and n <= 3:
            put.append((i, i, ("Wl", n)))
        if k == "aR":
            put.append((follow(prog, i, where[("aH", n)] - 1, LATE.get("aO", 0)), i, ("aO", n)))
        if after is None:
            continue
        if k in TRING:
            j = nth[it] + 3
            limit += ring[j:j + 1]
        last = min([where[x] for x in limit] + [len(prog)]) - 1
        put.append((follow(prog, i, last, LATE.get(after[0], 1)), i, after))
    put.sort()
    out = []
    for i, it in enumerate(prog):
        out.append(it)
        while put and put[0][0] == i:
            out.append(put.pop(0)[2])
    return out


def hybrid_block_kernel(nc, x_in, wqa, woa, wqb, wob, wg, wb, wl, bias_in, trig_in, iden_in,
                        mask_in, iota_in, out):
    prog = plan()

    tuse, guse, xuse = {}, {}, {}
    tfree, gfree, xfree = [], [], []
    for item in prog:
        k = item[0]
        if k in ("aT", "oT", "fT"):
            tuse[item] = len(tfree)
            tfree.append((k[0] + "l", item[1]))
            xuse[(k[0], item[1])] = len(xfree)
            xfree.append(({"a": "aK", "o": "oM", "f": "fB"}[k[0]], item[1]))
        elif k == "aS":
            tuse[item] = len(tfree)
            n, i = item[1:]
            tfree.append((f"kq{i}", n))
        elif k == "B":
            tuse[item] = len(tfree)
            tfree.append(("ex", 3 * item[1] + item[2]))
        elif k == "M2":
            tuse[item] = len(tfree)
            tfree.append(("mc", item[1]))
        elif k == "OT":
            tuse[item] = len(tfree)
            tfree.append(("on", item[1]))
        elif k == "fW":
            tuse[item] = len(tfree)
            tfree.append(("wl", item[1]))
        elif k in ("aQ", "aK", "oM", "fA", "fB") and item[2] == 0:
            guse[item[:2]] = len(gfree)
            gfree.append(({"aQ": "uq", "aK": "av", "oM": "ox", "fA": "fg", "fB": "fx"}[k], item[1]))

    with ExitStack() as ctx:
        def sb(name, shape, dt):
            return ctx.enter_context(nc.sbuf_tensor(name, shape, dt))

        def pb(name, shape):
            return ctx.enter_context(nc.psum_tensor(name, shape, F32))

        X = sb("X", [P, NT, D], F32)
        Wst = sb("Wst", [P, 1024], F32)
        WQh = sb("WQh", [P, 4, 768], F32R)
        WQl = sb("WQl", [P, 4, 768], F32R)
        WOh = sb("WOh", [P, 4, D], F32R)
        WOl = sb("WOl", [P, 4, D], F32R)
        WG = sb("WG", [P, 4, 272], F32R)
        WBh = sb("WBh", [P, 4, D], F32R)
        WBl = sb("WBl", [P, 4, D], F32R)
        WLh = sb("WLh", [P, D], F32R)
        WLl = sb("WLl", [P, D], F32R)
        xn = sb("xn", [P, 2, D], F32)
        at = sb("at", [P, 2, D], F32)
        XH = sb("XH", [P, 2, D], F32R)
        XL = sb("XL", [P, 2, D], F32R)
        U1 = sb("U1", [P, 2, 40, 8], F32)
        U2 = sb("U2", [P, 2, 40, 8], F32)
        Sst = sb("Sst", [P, 40, 64], F32R)
        QT = sb("QT", [P, 2, 4, 4, 2, 128], F32R)
        KT = sb("KT", [P, 2, 4, 3, 128], F32R)
        V = sb("V", [P, 2, 2, 8, 32], F32)
        PTs = sb("PTs", [P, 3, 3, 512], F32)
        Os = sb("Os", [P, 512], F32)
        rc = sb("rc", [P, 16], F32)
        nm = sb("nm", [P, 2, 2, 4, 2], F32)
        mhl = sb("mhl", [P, 2, 2, 8], F32R)
        mT = sb("mT", [32, 128], F32)
        st6 = sb("st6", [P, 2, 2, 6], F32)
        mv = sb("mv", [P, 2, 2, 2], F32)
        ve = sb("ve", [P, 2, 2], F32)
        rs = sb("rs", [P, 2, 2], F32)
        half = sb("half", [P, 2], F32)
        glo = sb("glo", [P, 2, 136], F32)
        mx = sb("mx", [P, 2, 8], F32)
        mi = sb("mi", [P, 2, 8], U32)
        gd = sb("gd", [P, 2], F32)
        gx = sb("gx", [P, 2], F32)
        gn = sb("gn", [P, 2], F32)
        wsel = sb("wsel", [P, 2, 2], F32)
        mif = sb("mif", [P, 2, 2], F32)
        t1 = sb("t1", [P, 2, 8], F32)
        t2 = sb("t2", [P, 2, 8], F32)
        wf = sb("wf", [P, 2, 8], F32)
        LH = sb("LH", [P, 256], F32R)
        LL = sb("LL", [P, 256], F32R)
        bias = sb("bias", [P, D], F32)
        trig = sb("trig", [P, 2, 4, 8], F32)
        iden = sb("iden", [P, 128], F32)
        mask = sb("mask", [P, 256], F32)
        iota = sb("iota", [P, 8], F32)

        SA = [pb(f"SA{i}", [P, 512]) for i in range(2)]
        T = [pb(f"T{i}", [P, 512]) for i in range(3)]
        O = pb("O", [P, 512])
        G = [pb(f"G{i}", [P, 512]) for i in range(2)]

        sems, made, known = {}, {}, {}

        def sem(name):
            if name not in sems:
                sems[name] = ctx.enter_context(nc.semaphore("s_" + name))
            return sems[name]

        def done(ins, name, n):
            assert made.get(name, 0) == n, (name, n, made.get(name))
            made[name] = n + 1
            ins.then_inc(sem(name), 1)

        def need(e, name, n, step=1):
            v = step * (n + 1)
            if n >= 0 and known.get((id(e), name), 0) < v:
                known[(id(e), name)] = v
                e.wait_ge(sem(name), v)

        def tbank(e, item):
            k = tuse[item]
            if k >= 3:
                need(e, *tfree[k - 3])
            return T[k % 3]

        def tb(item):
            return T[tuse[item] % 3]

        def gbank(e, key):
            k = guse[key]
            if k >= 2:
                need(e, *gfree[k - 2])
            return G[k % 2]

        def gb(key):
            return G[guse[key] % 2]

        def stack_out(e, copy, n, i):
            s, q = divmod(n, 2)
            need(e, "st", 5 * n + i)
            if s >= 2:
                need(e, "b", 3 * (8 * (s - 2) + 7) + 2)
            src = tb(("aS", n, i))[:, :].rearrange("p (g k) -> p g k", g=4)
            if i == 0:
                need(e, "kz", 1)
                for a in range(2):
                    ins = copy(KT[64 * a:64 * a + 64, s % 2, :, 2 if q else a, :], src[64 * a:64 * a + 64, :, :])
            else:
                ins = copy(QT[:, s % 2, i - 1, :, q, :], src)
            done(ins, f"kq{i}", n)

        def cols(dram, c, n):
            return dram[c * P:(c + 1) * P, 0:n]

        wch = []
        for c in range(4):
            wch.append((cols(wqa, c, 768), WQh[:, c, :], WQl[:, c, :], 768))
        for c in range(4):
            wch.append((cols(woa, c, D), WOh[:, c, :], WOl[:, c, :], D))
        for c in range(4):
            wch.append((cols(wg, c, 136), WG[:, c, 0:136], WG[:, c, 136:272], 136))
        for c in range(4):
            wch.append((cols(wb, c, D), WBh[:, c, :], WBl[:, c, :], D))
        wch.append((cols(wl, 0, D), WLh[:, :], WLl[:, :], D))
        for c in range(4):
            wch.append((cols(wqb, c, 768), WQh[:, c, :], WQl[:, c, :], 768))
        for c in range(4):
            wch.append((cols(wob, c, D), WOh[:, c, :], WOl[:, c, :], D))
        wland = [PTs[:, k // 2, :, :].rearrange("p a b -> p (a b)")[:, (k % 2) * 768:(k % 2 + 1) * 768]
                 if k < 4 else
                 Wst[:, 512 * (k % 2 if wch[k][3] < 768 else 0):][:, 0:wch[k][3]] for k in range(len(wch))]

        names = [it[1] for it in prog if it[0] == "W"]
        nw = len(wch)
        assert names[:nw] == list(range(nw))

        def wlanded(e, k):
            if k < 4:
                need(e, f"wf{k}", 0, 16)
            else:
                need(e, f"wd{k % 2}", (k - 4) // 2, 16)

        def split_low(e, k):
            need(e, "whi", k)
            if 17 <= k < 21:
                need(e, "aK", 15)
            if 21 <= k:
                need(e, "oM", 15)
            done(e.tensor_tensor(wch[k][2], wland[k], wch[k][1].bitcast(F32), ALU.subtract), "wlo", k)

        block = ctx.enter_context(nc.Block())

        @block.sync
        def _(e):
            def load(dst, src, name):
                e.dma_start(dst, src).then_inc(sem(name), 16)

            def xload(b):
                load(X[:, 2 * b:2 * b + 2, :],
                     x_in[256 * b:256 * b + 256, :].rearrange("(t p) d -> p t d", p=P), f"x{b}")

            for i in range(2):
                load(X[:, i, :], x_in[P * i:P * i + P, :], f"x0_{i}")
            load(iden[:, :], iden_in, "c_id")
            load(wland[0], wch[0][0], "wf0")
            load(wland[1], wch[1][0], "wf1")
            load(trig[:, :, :, :].rearrange("p a b c -> p (a b c)"), trig_in, "c_trig")
            load(wland[2], wch[2][0], "wf2")
            load(wland[3], wch[3][0], "wf3")
            load(mask[:, :], mask_in, "c_mask")
            for b in range(1, NB):
                xload(b)
            load(bias[:, :], bias_in, "c_bias")
            load(iota[:, :], iota_in, "c_iota")
            for k in (4, 5):
                load(wland[k], wch[k][0], f"wd{k % 2}")
            ready = []

            def store():
                while ready:
                    n = ready.pop(0)
                    need(e, "fx", n)
                    e.dma_start(out[(n - NT) * P:(n - NT + 1) * P, :], X[:, n - NT, :]).then_inc(sem("out"), 16)

            for item in prog:
                if item[0] == "W" and item[1] >= 4:
                    for k in range(6, nw):
                        if item[1] == (k - 1 if 17 <= k <= 21 else k - 2):
                            need(e, "wlo", item[1])
                            load(wland[k], wch[k][0], f"wd{k % 2}")
                elif item[0] == "M2":
                    p = item[1]
                    s, gg = divmod(p, 4)
                    need(e, "mc", p)
                    if s >= 2:
                        need(e, "b", 3 * (8 * (s - 2) + 7) + 2)
                    for a in range(2):
                        dst = QT[64 * a + 48:64 * a + 50, s % 2, gg, :, :, :].rearrange("r j q t -> r (j q t)").bitcast(F32)
                        e.dma_start(dst, mT[16 * a:16 * a + 16, :]).then_inc(sem("md"), 16)
                    store()
                elif item[0] == "fC" and item[1] >= NT:
                    ready.append(item[1])
            store()
            e.wait_ge(sem("out"), 16 * NT)


        @block.tensor
        def _(e):
            def front(c, n):
                item = (c + "T", n)
                if c == "o":
                    need(e, "on", 4 * (n // 2) + 3)
                    src = at[:, n % 2, :]
                else:
                    need(e, c + "xn", n)
                    src = xn[:, n % 2, :]
                need(e, "c_id", 0, 16)
                t = tbank(e, item)
                for k in range(4):
                    ins = e.transpose(t[:, k * P:(k + 1) * P], src[:, k * P:(k + 1) * P], iden[:, :])
                done(ins, c + "t", n)

            def chunk(c, key, n, j, width, wh, wlo, more=False):
                bank = gbank(e, (key, n)) if j == 0 else gb((key, n))
                k = xuse[(c, n)] % 2
                need(e, c + "h", n)
                need(e, c + "l", n)
                xh = XH[:, k, j * P:(j + 1) * P]
                xl = XL[:, k, j * P:(j + 1) * P]
                o = bank[:, 0:width]
                e.matmul(o, xh, wh, start=(j == 0), stop=False, skip_group_check=True)
                e.matmul(o, xh, wlo, start=False, stop=False, skip_group_check=True)
                ins = e.matmul(o, xl, wh, start=False, stop=(j == 3 and not more), skip_group_check=True)
                if j == 3:
                    done(ins, key, n)

            def v_aQ(n, j):
                need(e, "wlo", j if n < 16 else 17 + j)
                chunk("a", "aQ", n, j, 512, WQh[:, j, 0:512], WQl[:, j, 0:512])

            def v_aK(n, j):
                need(e, "wlo", j if n < 16 else 17 + j)
                chunk("a", "aK", n, j, 256, WQh[:, j, 512:768], WQl[:, j, 512:768])

            def v_aS(n, i):
                t = tbank(e, ("aS", n, i))
                for name in ("hq1", "lq", "lk"):
                    need(e, name, n)
                for j in range(4):
                    h = 32 + 2 * j if i == 0 else (i - 1) * 8 + 2 * j
                    src = Sst[:, h:h + 2, :].rearrange("p a b -> p (a b)").bitcast(F32)
                    ins = e.transpose(t[:, j * P:(j + 1) * P], src, iden[:, :])
                done(ins, "st", 5 * n + i)

            def ones(s, gg):
                for n in (2 * s, 2 * s + 1):
                    need(e, "kq0", n)
                    need(e, f"kq{gg + 1}", n)

            def v_A(u, i):
                s, g = divmod(u, 8)
                gg, r0 = g // 2, 64 * (g % 2)
                b, k = s % 2, 3 * u + i
                ones(s, gg)
                need(e, "m", k - 2)
                t = SA[k % 2]
                for j in range(2):
                    o = t[:, j * 256:(j + 1) * 256]
                    if i == 0:
                        ins = e.matmul(o.rearrange("p (a k) -> p a k", a=2),
                                       QT[0:112, b, gg, 2 * (u % 2) + j, 0, :], KT[0:112, b, gg, 0:2, :],
                                       start=True, stop=True, skip_group_check=True)
                    else:
                        ins = e.matmul(o.rearrange("p (a k) -> p a k", a=2),
                                       QT[r0:r0 + 48, b, gg, 2 * (i - 1) + j, 1, :],
                                       KT[r0:r0 + 48, b, gg, u % 2:3:2 - u % 2, :], start=True, stop=True,
                                       skip_group_check=True)
                done(ins, "sa", k)

            def v_M2(p):
                need(e, "ml", p)
                t = tbank(e, ("M2", p))
                done(e.transpose(t[0:32, 0:128], mhl[:, :, :, :].rearrange("p a h b -> p (a h b)").bitcast(F32),
                                 iden[:, :]), "mt", p)

            def v_B(u, i):
                s, g = divmod(u, 8)
                gg, r0 = g // 2, 64 * (g % 2)
                b = s % 2
                need(e, "md", u // 2, 32)
                t = tbank(e, ("B", u, i))
                kt = 2 if i == 2 else u % 2
                done(e.matmul(t[:, :].rearrange("p (j q) -> p j q", j=4),
                              KT[r0:r0 + 50, b, gg, kt, :],
                              QT[r0:r0 + 50, b, gg, :, min(i, 1), :], start=True, stop=True,
                              skip_group_check=True), "b", 3 * u + i)

            def v_PV(p):
                s = p // 4
                need(e, "ex", 6 * p + 5)
                need(e, "sel", 4 * p + 3)
                need(e, "av", 2 * s + 1)
                need(e, "vinit", 0)
                need(e, "oc", p - 1)
                for u in (2 * p, 2 * p + 1):
                    g, q = u % 8, 64 * (u % 2)
                    e.matmul(O[q:q + 32, :], V[:, s % 2, 0, g, :], PTs[:, u % 3, 0, :],
                             start=True, stop=True, skip_group_check=True)
                    e.matmul(O[q + 32:q + 64, :], V[:, s % 2, 0, g, :], PTs[:, u % 3, 1, :],
                             start=True, stop=False, skip_group_check=True)
                for u in (2 * p, 2 * p + 1):
                    g, q = u % 8, 64 * (u % 2)
                    ins = e.matmul(O[q + 32:q + 64, :], V[:, s % 2, 1, g, :], PTs[:, u % 3, 2, :],
                                   start=False, stop=True, skip_group_check=True)
                done(ins, "pv", p)

            def v_OT(p):
                need(e, "oc", p)
                t = tbank(e, ("OT", p))
                for j in range(4):
                    ins = e.transpose(t[:, j * P:(j + 1) * P], Os[:, j * P:(j + 1) * P], iden[:, :])
                done(ins, "oT", p)

            def v_oM(n, j):
                need(e, "wlo", 4 + j if n < 16 else 21 + j)
                chunk("o", "oM", n, j, 512, WOh[:, j, :], WOl[:, j, :])

            def v_fA(n, j):
                need(e, "wlo", 8 + j)
                t = gbank(e, ("fA", n)) if j == 0 else gb(("fA", n))
                k = xuse[("f", n)] % 2
                need(e, "fh", n)
                need(e, "fl", n)
                e.matmul(t[:, 0:272], XH[:, k, j * P:(j + 1) * P], WG[:, j, :], start=(j == 0), stop=False,
                         skip_group_check=True)
                ins = e.matmul(t[:, 136:272], XL[:, k, j * P:(j + 1) * P], WG[:, j, 0:136], start=False,
                               stop=(j == 3), skip_group_check=True)
                if j == 3:
                    done(ins, "fA", n)

            def v_fB(n, j):
                need(e, "wlo", 12 + j)
                chunk("f", "fB", n, j, 512, WBh[:, j, :], WBl[:, j, :], more=True)

            def v_fW(s):
                t = tbank(e, ("fW", s))
                for i in range(2):
                    need(e, "lw", 2 * s + i)
                    ins = e.transpose(t[:, i * P:(i + 1) * P], glo[:, i, 0:128], iden[:, :])
                done(ins, "wt", s)

            def v_fC(n):
                need(e, "wlo", 16)
                need(e, "wh", n // 2)
                need(e, "wl", n // 2)
                g = gb(("fB", n))
                i = n % 2
                e.matmul(g[:, :], LH[:, i * P:(i + 1) * P], WLh[:, :], start=False, stop=False,
                         skip_group_check=True)
                e.matmul(g[:, :], LH[:, i * P:(i + 1) * P], WLl[:, :], start=False, stop=False,
                         skip_group_check=True)
                done(e.matmul(g[:, :], LL[:, i * P:(i + 1) * P], WLh[:, :], start=False, stop=True,
                              skip_group_check=True), "fC", n)

            for item in prog:
                k, a = item[0], item[1:]
                if k in ("aT", "oT", "fT"):
                    front(k[0], *a)
                elif k == "aQ":
                    v_aQ(*a)
                elif k == "aK":
                    v_aK(*a)
                elif k == "aS":
                    v_aS(*a)
                elif k == "A":
                    v_A(*a)
                elif k == "M2":
                    v_M2(*a)
                elif k == "B":
                    v_B(*a)
                elif k == "PV":
                    v_PV(*a)
                elif k == "OT":
                    v_OT(*a)
                elif k == "oM":
                    v_oM(*a)
                elif k == "fA":
                    v_fA(*a)
                elif k == "fB":
                    v_fB(*a)
                elif k == "fW":
                    v_fW(*a)
                elif k == "fC":
                    v_fC(*a)

        @block.scalar
        def _(e):
            def copy(dst, src):
                return e.activation(dst, src, ACT.Copy)

            def front_h(c, n):
                k = xuse[(c, n)]
                need(e, c + "t", n)
                if k >= 2:
                    need(e, *xfree[k - 2])
                done(copy(XH[:, k % 2, :], tb((c + "T", n))[:, :]), c + "h", n)

            def s_W(k):
                wlanded(e, k)
                if 17 <= k < 21:
                    need(e, "aK", 15)
                if 21 <= k:
                    need(e, "oM", 15)
                n = wch[k][3]
                done(copy(wch[k][1], wland[k]), "whi", k)

            def s_aV(n):
                need(e, "uk", n)
                s = n // 2
                if s >= 2:
                    need(e, "pv", 4 * (s - 2) + 3)
                need(e, "vinit", 0)
                done(copy(V[:, s % 2, n % 2, :, 0:16],
                          gb(("aK", n))[:, 128:256].rearrange("p (g d) -> p g d", d=16)), "av", n)

            def s_aH(n):
                need(e, "ro", n)
                need(e, "st", 5 * (n - 1) + 4)
                need(e, "sinit", 0)
                for r in range(2):
                    done(copy(Sst[:, 0:32, 32 * r:32 * r + 16].rearrange("p a (h f) -> p h a f", h=2),
                              U1[:, :, 0:32, :]), f"hq{r}", n)
                for r in range(2):
                    done(copy(Sst[:, 32:40, 16 * r:16 * r + 16].rearrange("p a (h f) -> p h a f", h=2),
                              U1[:, :, 32:40, :]), f"hk{r}", n)

            def s_aS(n, i):
                stack_out(e, copy, n, i)

            def s_M2(p):
                need(e, "mt", p)
                need(e, "md", p - 1, 32)
                done(copy(mT[:, :], tb(("M2", p))[0:32, 0:128]), "mc", p)

            def s_B(u, i):
                need(e, "b", 3 * u + i)
                if u >= 3:
                    need(e, "pv", (u - 3) // 2)
                else:
                    need(e, "wlo", 3)
                done(e.activation(PTs[:, u % 3, i, :], tb(("B", u, i))[:, :], ACT.Exp), "ex", 3 * u + i)

            def s_PV(p):
                need(e, "pv", p)
                need(e, "oT", p - 1)
                done(copy(Os[:, :], O[:, :]), "oc", p)

            def s_fA(n, j):
                if j == 3:
                    need(e, "fA", n)
                    need(e, "wt", n // 2 - 1)
                    done(copy(glo[:, n % 2, :], gb(("fA", n))[:, 0:136]), "fe", n)

            def s_fG(s):
                need(e, "gd", s)
                done(e.activation(gx[:, :], gd[:, :], ACT.Exp), "gx", s)

            def s_fW(s):
                need(e, "wt", s)
                need(e, "fC", 2 * s - 1)
                done(copy(LH[:, :], tb(("fW", s))[:, 0:256]), "wh", s)

            for item in prog:
                k, a = item[0], item[1:]
                if k == "W":
                    s_W(*a)
                elif k in ("aT", "oT", "fT"):
                    front_h(k[0], *a)
                elif k == "aV":
                    s_aV(*a)
                elif k == "aH":
                    s_aH(*a)
                elif k == "aS":
                    s_aS(*a)
                elif k == "M2":
                    s_M2(*a)
                elif k == "B":
                    s_B(*a)
                elif k == "PV":
                    s_PV(*a)
                elif k == "fA":
                    s_fA(*a)
                elif k == "fG":
                    s_fG(*a)
                elif k == "fW":
                    s_fW(*a)

        @block.vector
        def _(e):
            def front_l(c, n):
                k = xuse[(c, n)]
                need(e, c + "h", n)
                if k >= 2:
                    need(e, *xfree[k - 2])
                done(e.tensor_tensor(XL[:, k % 2, :], tb((c + "T", n))[:, :], XH[:, k % 2, :].bitcast(F32),
                                     ALU.subtract), c + "l", n)

            def stats(c, n):
                w, i, t = int(c == "f"), n % 2, n % NT
                if c == "f":
                    need(e, "ox", n)
                elif n < 2:
                    need(e, f"x0_{n}", 0, 16)
                elif n < NT:
                    need(e, f"x{n // 2}", 0, 16)
                else:
                    need(e, "fx", n - NT)
                done(e.bn_stats(st6[:, w, i, :], X[:, t, :]), "nb" + c, n)
                need(e, "nb" + c, n)
                done(e.bn_aggr(mv[:, w, i, :], st6[:, w, i, :]), "ng" + c, n)
                need(e, "ng" + c, n)
                need(e, "np" + c, n - 2)
                done(e.tensor_scalar(ve[:, w, i:i + 1], mv[:, w, i, 1:2], EPS, None, ALU.add), "ne" + c, n)

            def norm(c, n):
                w, i, t = int(c == "f"), n % 2, n % NT
                need(e, "np" + c, n)
                need(e, *lnfree[(c, n)])
                done(e.tensor_scalar(xn[:, i, :], X[:, t, :], mv[:, w, i, 0:1], rs[:, w, i:i + 1],
                                     ALU.subtract, ALU.mult), c + "xn", n)

            lnfree, last = {}, {}
            for it in prog:
                if it[0] in ("aN", "fN"):
                    c, n = it[0][0], it[1]
                    lnfree[(c, n)] = last.get(n % 2, ("at", -1))
                    last[n % 2] = (c + "t", n)

            def v_aR(n):
                q = n % 2
                need(e, "c_trig", 0, 16)
                need(e, "aQ", n)
                need(e, "hk1", n - 1)
                need(e, "lk", n - 1)
                g = gb(("aQ", n))[:, :].rearrange("p (h a f) -> p h a f", h=2, f=8)

                def tr(i, h):
                    return trig[:, q, i, :].unsqueeze(1).unsqueeze(1).to_broadcast([P, 2, h, 8])

                e.tensor_tensor(U1[:, :, 0:32, :], g, tr(0, 32), ALU.mult)
                done(e.tensor_tensor(U2[:, :, 0:32, :], g, tr(1, 32), ALU.mult), "uq", n)
                need(e, "aK", n)
                g = gb(("aK", n))[:, 0:128].rearrange("p (h a f) -> p h a f", h=2, f=8)
                e.tensor_tensor(U1[:, :, 32:40, :], g, tr(2, 8), ALU.mult)
                done(e.tensor_tensor(U2[:, :, 32:40, :], g, tr(3, 8), ALU.mult), "uk", n)

            def v_A(u, i):
                p, k = u // 2, 3 * u + i
                need(e, "sa", k)
                if i == 0:
                    need(e, "ml", p - 2)
                need(e, "c_mask", 0, 16)
                w = 128 if i == 0 else 256
                for j in range(512 // w):
                    a, h = (j % 2, 2 * (u % 2) + j // 2) if i == 0 else (u % 2, 2 * (i - 1) + j)
                    x = SA[k % 2][:, j * w:(j + 1) * w]
                    ins = e.tensor_tensor_reduce(x, x, mask[:, 256 - w:256], 1.0, LOWEST, ALU.add, ALU.max,
                                                 nm[:, p % 2, a, h, min(i, 1):min(i, 1) + 1])
                done(ins, "m", k)

            def v_M1(p):
                src = nm[:, p % 2, :, :, :].rearrange("p a j q -> p a (j q)")
                need(e, "m", 6 * p + 5)
                need(e, "mt", p - 1)
                done(e.tensor_copy(mhl[:, :, 0, :], src), "mh", p)
                need(e, "mh", p)
                done(e.tensor_tensor(mhl[:, :, 1, :], src, mhl[:, :, 0, :].bitcast(F32), ALU.subtract), "ml", p)

            def v_OT(p):
                s, gg = divmod(p, 4)
                need(e, "oT", p)
                need(e, "ot", 2 * s - 1)
                t = tb(("OT", p))[:, :].rearrange("p (j a q d) -> p j a q d", j=4, a=2, q=2)
                need(e, "on", p - 1)
                done(e.reciprocal(rc[:, :].rearrange("p (j a q) -> p j a q", j=4, a=2), t[:, :, :, :, 16]),
                     "rc", p)
                need(e, "rc", p)
                for q in range(2):
                    dst = at[:, q, gg * 128:(gg + 1) * 128].rearrange("p (a j d) -> p j a d", a=2, j=4)
                    rb = rc[:, :].rearrange("p (j a q) -> p j a q", j=4, a=2)[:, :, :, q]
                    ins = e.tensor_tensor(dst, t[:, :, :, q, 0:16],
                                          rb.unsqueeze(3).to_broadcast([P, 4, 2, 16]), ALU.mult)
                done(ins, "on", p)

            def v_oM(n, j):
                if j < 3:
                    return
                t = n % NT
                need(e, "oM", n)
                done(e.tensor_tensor(X[:, t, :], gb(("oM", n))[:, :], X[:, t, :], ALU.add), "ox", n)

            def v_fE(n):
                t = gb(("fA", n))
                need(e, "fe", n)
                done(e.tensor_tensor(glo[:, n % 2, :], t[:, 136:272], glo[:, n % 2, :], ALU.add), "fg", n)

            def v_fG(s):
                need(e, "c_iota", 0, 16)
                for i in range(2):
                    n = 2 * s + i
                    need(e, "fg", n)
                    lg = glo[:, i, 128:136]
                    done(e.max(mx[:, i, :], lg), "mx", n)
                for i in range(2):
                    n = 2 * s + i
                    need(e, "mx", n)
                    done(e.max_index(mi[:, i, :], mx[:, i, :], glo[:, i, 128:136]), "mi", n)
                need(e, "gx", s - 1)
                done(e.tensor_tensor(gd[:, :], mx[:, :, 1], mx[:, :, 0], ALU.subtract), "gd", s)
                need(e, "mi", 2 * s + 1)
                done(e.tensor_copy(mif[:, :, :], mi[:, :, 0:2]), "mif", s)

            def v_fH(s):
                need(e, "gx", s)
                done(e.tensor_scalar(gn[:, :], gx[:, :], 1.0, None, ALU.add), "gn", s)
                need(e, "gn", s)
                done(e.reciprocal(wsel[:, :, 0], gn[:, :]), "w0", s)
                need(e, "w0", s)
                done(e.tensor_tensor(wsel[:, :, 1], gx[:, :], wsel[:, :, 0], ALU.mult), "w1", s)
                need(e, "w1", s)
                need(e, "mif", s)
                for i in range(2):
                    n = 2 * s + i
                    done(e.tensor_scalar(t1[:, i, :], iota[:, :], mif[:, i, 0:1], wsel[:, i, 0:1],
                                         ALU.is_equal, ALU.mult), "ta", n)
                    done(e.tensor_scalar(t2[:, i, :], iota[:, :], mif[:, i, 1:2], wsel[:, i, 1:2],
                                         ALU.is_equal, ALU.mult), "tb", n)
                need(e, "tb", 2 * s + 1)
                done(e.tensor_tensor(wf[:, :, :], t1[:, :, :], t2[:, :, :], ALU.add), "wf", s)
                need(e, "wf", s)
                need(e, "wt", s - 1)
                for i in range(2):
                    n = 2 * s + i
                    done(e.scalar_tensor_tensor(
                        glo[:, i, 0:128].rearrange("p (a r) -> p a r", r=16),
                        glo[:, i, 0:128].rearrange("p (a r) -> p a r", r=16), SCALING,
                        wf[:, i, :].unsqueeze(2).to_broadcast([P, 8, 16]), ALU.mult, ALU.mult), "lw", n)

            def v_fW(s):
                need(e, "wh", s)
                need(e, "fC", 2 * s - 1)
                done(e.tensor_tensor(LL[:, :], tb(("fW", s))[:, 0:256], LH[:, :].bitcast(F32), ALU.subtract),
                     "wl", s)

            def v_fC(n):
                t = n % NT
                need(e, "fC", n)
                need(e, "xb", n)
                done(e.tensor_tensor(X[:, t, :], gb(("fB", n))[:, :], X[:, t, :], ALU.add), "fx", n)

            for item in prog:
                k, a = item[0], item[1:]
                if k == "Wl" and a[0] < 4:
                    split_low(e, *a)
                elif k in ("aL", "fL"):
                    stats(k[0], *a)
                elif k in ("aN", "fN"):
                    norm(k[0], *a)
                elif k == "xL":
                    front_l(*a)
                elif k == "aR":
                    v_aR(*a)
                elif k == "A":
                    v_A(*a)
                elif k == "M1":
                    v_M1(*a)
                elif k == "OT":
                    v_OT(*a)
                elif k == "oM":
                    v_oM(*a)
                elif k == "fE":
                    v_fE(*a)
                elif k == "fG":
                    v_fG(*a)
                elif k == "fH":
                    v_fH(*a)
                elif k == "fV":
                    v_fW(*a)
                elif k == "fC":
                    v_fC(*a)

        @block.gpsimd
        def _(e):
            done(e.memset(half[:, :], -0.5), "half", 0)
            need(e, "half", 0)
            def power(c, n):
                w, i = int(c == "f"), n % 2
                need(e, "ne" + c, n)
                need(e, c + "xn", n - 2)
                done(e.tensor_tensor(rs[:, w, i:i + 1], ve[:, w, i:i + 1], half[:, 0:1], ALU.pow), "np" + c, n)

            def addbias(n):
                need(e, "c_bias", 0, 16)
                need(e, "fxn", n)
                t = n % NT
                done(e.tensor_tensor(X[:, t, :], X[:, t, :], bias[:, :], ALU.add), "xb", n)

            def causal(u, i):
                blk = PTs[:, u % 3, i, :].rearrange("p (j q) -> p j q", j=4)
                need(e, "ex", 3 * u + i)
                done(e.affine_select(out=blk, in_=blk, compare_op=ALU.is_ge, fill=0.0, base=0,
                                     pattern=[[0, 4], [1, 128]], channel_multiplier=-1), "sel", 2 * u + i // 2)

            def p_aO(n):
                need(e, "uk", n)
                e.tensor_tensor(U1[:, 0, :, :], U1[:, 0, :, :], U2[:, 1, :, :], ALU.subtract)
                done(e.tensor_tensor(U1[:, 1, :, :], U1[:, 1, :, :], U2[:, 0, :, :], ALU.add), "ro", n)

            def p_aZ(n):
                need(e, "ro", n)
                need(e, "hq0", n)
                done(e.tensor_tensor(Sst[:, 0:32, 16:32].rearrange("p a (h f) -> p h a f", h=2),
                                     U1[:, :, 0:32, :],
                                     Sst[:, 0:32, 0:16].rearrange("p a (h f) -> p h a f", h=2).bitcast(F32),
                                     ALU.subtract), "lq", n)
                need(e, "hk0", n)
                need(e, "hk1", n)
                done(e.tensor_tensor(Sst[:, 32:40, 32:48].rearrange("p a (h f) -> p h a f", h=2),
                                     U1[:, :, 32:40, :],
                                     Sst[:, 32:40, 0:16].rearrange("p a (h f) -> p h a f", h=2).bitcast(F32),
                                     ALU.subtract), "lk", n)

            def clear():
                done(e.memset(Sst[:, :, :].bitcast(F32), 0.0), "sz", 0)
                for a in range(2):
                    done(e.memset(KT[64 * a:64 * a + 64, :, :, 1 - a, :].bitcast(F32), 0.0), "kz", a)
                    need(e, "kz", a)
                need(e, "sz", 0)
                done(e.memset(Sst[:, 32:40, 48:50].bitcast(F32), -1.0), "sinit", 0)
                done(e.memset(V[:, :, :, :, :], 0.0), "vz", 0)
                need(e, "vz", 0)
                done(e.memset(V[:, :, :, :, 16:17], 1.0), "vinit", 0)

            for item in prog:
                if item[0] == "aO":
                    p_aO(item[1])
                if item[0] == "aZ":
                    need(e, "sinit", 0)
                    p_aZ(item[1])
                if item[0] == "Wl" and item[1] >= 4:
                    need(e, "wlo", 3)
                    split_low(e, item[1])
                if item[0] == "B" and item[2] != 1:
                    causal(*item[1:])
                if item[0] in ("aL", "fL"):
                    power(item[0][0], item[1])
                if item == ("aL", 1):
                    clear()
                if item[0] == "fN":
                    addbias(item[1])


_IN = ["x", "wqa", "woa", "wqb", "wob", "wg", "wb", "wl", "bias", "trig", "iden", "mask", "iota"]


def kernel(L0_attn_a_x, L0_attn_a_w_qkv, L0_attn_a_w_o, L0_attn_b_wq, L0_attn_b_wk, L0_attn_b_wv,
           L0_attn_b_wo, L0_ffn_gate_w, L0_ffn_base_w, L0_ffn_base_b, L0_ffn_lora_A, L0_ffn_lora_B):
    import numpy as np
    import concourse.bacc as bacc
    from concourse.bass_utils import run_bass_kernel_spmd

    def lay(w):
        w = np.asarray(w)
        q = w[:, 0:512].reshape(512, 4, 2, 4, 8, 2).transpose(0, 5, 1, 3, 2, 4).reshape(512, 512)
        k = w[:, 512:640].reshape(512, 8, 8, 2).transpose(0, 3, 1, 2).reshape(512, 128)
        return np.ascontiguousarray(np.concatenate([q, k, w[:, 640:768]], axis=1))

    f = np.float32
    freq = f(1.0) / f(10000.0) ** (np.arange(0, 16, 2, dtype=f) / f(16))
    ang = np.arange(256, dtype=f)[:, None] * freq[None, :]
    c, s = np.cos(ang).astype(f), np.sin(ang).astype(f)
    trig = np.stack([c * f(0.25), s * f(0.25), c, s], axis=1).reshape(2, 128, 4, 8).transpose(1, 0, 2, 3)
    tri = np.where(np.arange(128)[None, :] > np.arange(128)[:, None], f(-1e30), f(0))
    arrays = {
        "x": np.ascontiguousarray(np.asarray(L0_attn_a_x).reshape(2048, 512)),
        "wqa": lay(L0_attn_a_w_qkv),
        "woa": np.ascontiguousarray(L0_attn_a_w_o),
        "wqb": lay(np.concatenate([np.asarray(L0_attn_b_wq), np.asarray(L0_attn_b_wk),
                                   np.asarray(L0_attn_b_wv)], axis=1)),
        "wob": np.ascontiguousarray(L0_attn_b_wo),
        "wg": np.ascontiguousarray(np.concatenate([np.asarray(L0_ffn_lora_A).reshape(128, 512).T,
                                                   np.asarray(L0_ffn_gate_w).T], axis=1)),
        "wb": np.ascontiguousarray(np.asarray(L0_ffn_base_w).T),
        "wl": np.ascontiguousarray(np.asarray(L0_ffn_lora_B).transpose(0, 2, 1).reshape(128, 512)),
        "bias": np.ascontiguousarray(np.broadcast_to(np.asarray(L0_ffn_base_b)[None, :], (128, 512))),
        "trig": np.ascontiguousarray(trig.reshape(128, 64)),
        "iden": np.eye(128, dtype=f),
        "mask": np.ascontiguousarray(np.concatenate([np.zeros((128, 128), f), tri], axis=1)),
        "iota": np.ascontiguousarray(np.broadcast_to(np.arange(8, dtype=f)[None, :], (128, 8))),
    }
    nc = bacc.Bacc("TRN2", target_bir_lowering=False, num_devices=1)
    args = [nc.dram_tensor("in_" + n, arrays[n].shape, mybir.dt.from_np(arrays[n].dtype),
                           kind="ExternalInput").ap() for n in _IN]
    out = nc.dram_tensor("out_0", (2048, 512), F32, kind="ExternalOutput").ap()
    hybrid_block_kernel(nc, *args, out)
    r = run_bass_kernel_spmd(nc, [{"in_" + n: a for n, a in arrays.items()}], core_ids=[0])
    return r.results[0]["out_0"].reshape(8, 256, 512)
```
